# Optimizing a Trainium2 kernel written in Bass

```python
import numpy as np
import jax
import jax.numpy as jnp

def _softmax(x, axis=-1):
    return jax.nn.softmax(x, axis=axis)

def _gelu(x):
    return jax.nn.gelu(x, approximate=True)

def _silu(x):
    return jax.nn.silu(x)

def _sigmoid(x):
    return jax.nn.sigmoid(x)

def _layernorm(x, axis=-1, eps=1e-05):
    m = jnp.mean(x, axis=axis, keepdims=True)
    v = jnp.var(x, axis=axis, keepdims=True)
    return (x - m) / jnp.sqrt(v + eps)

def _scatter_add(tgt, idx, src, axis=0):
    return tgt.at[idx].add(src)

def _segment_sum(src, seg, n):
    return jax.ops.segment_sum(src, seg, n)
kernel_name = 'mk_gnn_resnorm_d1_gnn_r8_f6d5a4'

def setup_inputs(seed: int=0):
    np.random.seed(seed)
    _w = jnp.asarray

    def _rec_inputs():
        import jax
        import jax.numpy as jnp
        _gk = jax.random.key(seed)
        x = -0.000202 + 1 * jax.random.normal(jax.random.fold_in(_gk, 1), (6250, 128), jnp.float32)
        _s = jax.random.randint(jax.random.fold_in(_gk, 2), (50000,), 0, 6250, jnp.int32)
        _d = jax.random.randint(jax.random.fold_in(_gk, 3), (50000,), 0, 6250, jnp.int32)
        _loop = jnp.arange(6250, dtype=jnp.int32)
        src = jnp.concatenate([_s, _d, _loop])
        dst = jnp.concatenate([_d, _s, _loop])
        _o = jnp.argsort(dst, stable=True)
        src = src[_o]
        dst = dst[_o]
        edge_type_3 = jax.random.randint(jax.random.fold_in(_gk, 12), (106250,), 0, 3, jnp.int32)
        node_type_3 = jax.random.randint(jax.random.fold_in(_gk, 13), (6250,), 0, 3, jnp.int32)
        return (x, src, dst, edge_type_3, node_type_3)
    x, src, dst, edge_type_3, node_type_3 = _rec_inputs()

    def _L0_gnn_setup():
        import jax, jax.numpy as jnp
        import numpy as np
        N_NODES = 6250
        N_EDGES = 100000
        D = 128
        T = 3
        NODE_IN = D + T * D
        key = jax.random.key(seed)
        ks = jax.random.split(key, 8)
        scale = 0.05
        return {'node_feature': jax.random.normal(ks[0], (N_NODES, D), jnp.float32), 'W_e': jax.random.normal(ks[1], (T, D, D), jnp.float32) * scale, 'b_e': jnp.zeros((T, D), jnp.float32), 'W_n': jax.random.normal(ks[2], (T, D, NODE_IN), jnp.float32) * scale, 'b_n': jnp.zeros((T, D), jnp.float32), 'edge_src': jax.random.randint(ks[3], (N_EDGES,), 0, N_NODES, jnp.int32), 'edge_dst': jax.random.randint(ks[4], (N_EDGES,), 0, N_NODES, jnp.int32), 'edge_type': jax.random.randint(ks[5], (N_EDGES,), 0, T, jnp.int32), 'node_type': jax.random.randint(ks[6], (N_NODES,), 0, T, jnp.int32)}
    _L0_gnn_all = _L0_gnn_setup()
    _L0_gnn_in = {k: v for k, v in _L0_gnn_all.items() if k in ('W_e', 'b_e', 'W_n', 'b_n')}
    del _L0_gnn_all
    return {'x': x, 'src': src, 'dst': dst, 'edge_type_3': edge_type_3, 'node_type_3': node_type_3, 'L0_gnn_W_e': _L0_gnn_in['W_e'], 'L0_gnn_b_e': _L0_gnn_in['b_e'], 'L0_gnn_W_n': _L0_gnn_in['W_n'], 'L0_gnn_b_n': _L0_gnn_in['b_n']}

def reference(x, src, dst, edge_type_3, node_type_3, L0_gnn_W_e, L0_gnn_b_e, L0_gnn_W_n, L0_gnn_b_n):
    import jax
    import jax.numpy as jnp

    def _L0_gnn_ref(node_feature, W_e, b_e, W_n, b_n, edge_src, edge_dst, edge_type, node_type):
        import jax, jax.numpy as jnp
        import numpy as np
        N_NODES = 6250
        N_EDGES = 100000
        D = 128
        T = 3
        NODE_IN = D + T * D
        N, Din = node_feature.shape
        n_types = W_e.shape[0]
        out_dim = W_e.shape[1]
        src = node_feature[edge_src]
        parts = [jax.nn.relu(node_feature)]
        for t in range(n_types):
            msg = jax.nn.relu(src @ W_e[t].T + b_e[t])
            msg = jnp.where((edge_type == t)[:, None], msg, jnp.zeros((), msg.dtype))
            parts.append(jax.ops.segment_sum(msg, edge_dst, num_segments=N))
        agg = jnp.concatenate(parts, axis=1)
        updated = jnp.zeros((N, out_dim), node_feature.dtype)
        for t in range(n_types):
            o = agg @ W_n[t].T + b_n[t]
            updated = jnp.where((node_type == t)[:, None], o, updated)
        return updated + node_feature
    x = _layernorm(x + _L0_gnn_ref(x, L0_gnn_W_e, L0_gnn_b_e, L0_gnn_W_n, L0_gnn_b_n, src, dst, edge_type_3, node_type_3), axis=-1)
    return x

_drawn_inputs = setup_inputs


def setup_inputs(seed=0):
    import zlib

    import numpy as np

    out = dict(_drawn_inputs(seed))
    spreads = {'L0_gnn_b_e': (0.0, 0.1), 'L0_gnn_b_n': (0.0, 0.1)}
    factors = {}
    for name, (base, spread) in spreads.items():
        noise = np.random.default_rng([zlib.crc32(name.encode()), seed]).standard_normal(out[name].shape)
        drawn = base * np.exp(spread * noise) if base else spread * noise
        out[name] = jnp.asarray(drawn.astype(out[name].dtype))
    for name, factor in factors.items():
        out[name] = (out[name] * factor).astype(out[name].dtype)
    return out
```

```python
from contextlib import ExitStack

import concourse.bass as bass
from concourse import mybir

F32 = mybir.dt.float32
I32 = mybir.dt.int32
ALU = mybir.AluOpType
ACT = mybir.ActivationFunctionType
AX = mybir.AxisListType

P = 128
N, D, T, E = 6250, 128, 3, 106250
EPS = 1e-5

NT = -(-N // P)
TAIL = N - (NT - 1) * P
CT = -(-E // (NT * P))
ROW = CT * P
LAST = E - (NT - 1) * ROW
SIZES = [4, 4, 3, 3, 3]
assert sum(SIZES) == CT
NG = len(SIZES)
FIRST = [sum(SIZES[:g]) for g in range(NG)]
LAST_CT = -(-LAST // P)
LAST_SIZES = [max(0, min(SIZES[g], LAST_CT - FIRST[g])) for g in range(NG)]
assert min(LAST_SIZES) > 0
FIN = 2
WIN = 42
TYPE_STEP = 16384
assert TYPE_STEP > 2 * N + WIN
NPAD = N + WIN
ST = NG + 2

XB = 4
NB = (NT - 1) // XB
assert NB * XB == NT - 1 and NB % 2 == 0

AGG, FPS, XPS = 0, 5, 6
SETUP_BANKS = 6
MSG_PS, XT_PS = 1, (6, 7)


def build(nc, x, src, dst, etype, ntype, w_e, b_e, w_n, b_n, out):
    table = nc.dram_tensor("message_table", [N * T, D], F32, kind="Internal").ap()
    stats_dram = nc.dram_tensor("stats_row", [NT * ST], F32, kind="Internal").ap()

    with ExitStack() as ctx:
        def sb(name, shape, dt=F32):
            return ctx.enter_context(nc.sbuf_tensor(name, shape, dt))

        def sem(name):
            return ctx.enter_context(nc.semaphore(name))

        acc = sb("acc", [P, T, NPAD])
        src_raw = sb("src_raw", [NT, ROW], I32)
        dst_raw = sb("dst_raw", [NT, ROW], I32)
        typ_raw = sb("typ_raw", [NT, ROW], I32)
        idx_f = sb("idx_f", [NT, ROW])
        key_f = sb("key_f", [NT, ROW])
        idx_t = sb("idx_t", [P, NT, CT], I32)
        key_t = sb("key_t", [P, NT, CT])
        idx_ring = sb("idx_ring", [P, CT], I32)
        msg = sb("msg", [P, CT, D])
        hot = sb("hot", [P, CT, T * WIN])
        hot_iota = sb("hot_iota", [P, T * WIN])
        stats = sb("stats", [NT, ST])
        top = sb("top", [NT, 2 * NG])
        limit = sb("limit", [NT, NG])
        row_f = sb("row_f", [1, NT * ST])
        row_i = sb("row_i", [1, NT * ST], I32)
        ctl_f = sb("ctl_f", [1, 6])
        ctl = sb("ctl", [1, 2], I32)
        xin = sb("xin", [P, 2, XB, D])
        xt = sb("xt", [P, 2, XB, P])
        tab = sb("tab", [P, 2, XB, T * D])
        we_raw = sb("we_raw", [P, T, D])
        wn_raw = sb("wn_raw", [P, T, (T + 1) * D])
        we_t = sb("we_t", [P, T * D])
        wn_t = sb("wn_t", [P, T + 1, T * D])
        be_b = sb("be_b", [P, T * D])
        bn_row = sb("bn_row", [1, T * D])
        ones = sb("ones", [1, P])
        ident = sb("ident", [P, P])
        nt_raw = sb("nt_raw", [NT, P], I32)
        nt_f = sb("nt_f", [NT, P])
        nt_t = sb("nt_t", [P, NT])
        mask = sb("mask", [P, T, NT])
        x_fin = sb("x_fin", [P, D])
        stage = sb("stage", [P, T + 1, P])
        h = sb("h", [P, D])
        y = sb("y", [P, D])
        bnst = sb("bnst", [P, 6])
        mv = sb("mv", [P, 2])
        sd = sb("sd", [P, 1])
        rstd = sb("rstd", [P, 1])
        eps = sb("eps", [P, 1])
        ps = ctx.enter_context(nc.psum_tensor("ps", [P, 8, 512], F32))

        got_edges, got_we, got_wn, got_bias = sem("got_edges"), sem("got_we"), sem("got_wn"), sem("got_bias")
        got_nt = sem("got_nt")
        got_x = [sem("got_x0"), sem("got_x1")]
        pads_set, ident_set, consts_set = sem("pads_set"), sem("ident_set"), sem("consts_set")
        hot_iota_set, acc_zeroed, limits_set = sem("hot_iota_set"), sem("acc_zeroed"), sem("limits_set")
        nt_cast, masks_set = sem("nt_cast"), sem("masks_set")
        minmax_set, stats_set, prep_step, keys_set = (sem("minmax_set"), sem("stats_set"), sem("prep_step"),
                                                      sem("keys_set"))
        stats_out, stats_in, ctl_set = sem("stats_out"), sem("stats_in"), sem("ctl_set")
        setup_t, setup_copied = sem("setup_t"), sem("setup_copied")
        vec_step = sem("vec_step")
        x_turned, xt_copied, msg_made = sem("x_turned"), sem("xt_copied"), sem("msg_made")
        biased, tab_ready = sem("biased"), sem("tab_ready")
        tab_stored = [sem("tab_stored0"), sem("tab_stored1")]
        hot_ready, idx_ready = sem("hot_ready"), sem("idx_ready")
        gathered = [sem(f"gathered{g}") for g in range(NG)]
        group_summed, group_added = sem("group_summed"), sem("group_added")
        fin_x, fin_xt, stage_xt, stage_acc, fin_lin = (sem("fin_x"), sem("fin_xt"), sem("stage_xt"),
                                                       sem("stage_acc"), sem("fin_lin"))
        fin_step, fin_var, fin_sd, fin_y, stored = (sem("fin_step"), sem("fin_var"), sem("fin_sd"),
                                                    sem("fin_y"), sem("stored"))
        FIN_STEPS = 6
        gen_shift, gen_ready, gen_summed, gen_added, gen_done = (
            sem("gen_shift"), sem("gen_ready"), sem("gen_summed"), sem("gen_added"), sem("gen_done"))
        gen_gathered = [sem(f"gen_gathered{g}") for g in range(NG)]
        SHIFTS = 3

        UNITS = ([("we", T, P)] + [("wn", T, P)] * (T + 1) + [("nt", 1, NT)]
                 + [("key", 10, NT), ("key", CT - 10, NT), ("idx", 10, NT), ("idx", CT - 10, NT)])
        EDGE_UNIT = T + 3

        block = ctx.enter_context(nc.Block())

        def hold(engine):
            engine.nop(nofuse=True)

        @block.sync
        def _(sp):
            sp.dma_start(we_raw[:, :, :], w_e.rearrange("t o i -> o t i")).then_inc(got_we, 16)

            def load_x(b, par):
                sp.dma_start(xin[:, par, :, :],
                             x[bass.ds(b * (XB * P), XB * P), :].rearrange("(j p) d -> p j d", p=P)
                             ).then_inc(got_x[par], 16)
            load_x(0, 0)
            load_x(1, 1)
            sp.wait_ge(pads_set, 4)
            for raw, dram in ((dst_raw, dst), (src_raw, src), (typ_raw, etype)):
                sp.dma_start(raw[0:NT - 1, :], dram[0:(NT - 1) * ROW].rearrange("(p c) -> p c", c=ROW)
                             ).then_inc(got_edges, 16)
                sp.dma_start(raw[NT - 1:NT, 0:LAST], dram[(NT - 1) * ROW:E].rearrange("(p c) -> p c", p=1)
                             ).then_inc(got_edges, 16)
            sp.dma_start(be_b[:, :], b_e.rearrange("(a t) o -> a (t o)", a=1).broadcast_to((P, T * D))
                         ).then_inc(got_bias, 16)
            sp.dma_start(bn_row[:, :], b_n.rearrange("(a t) o -> a (t o)", a=1)).then_inc(got_bias, 16)
            sp.dma_start(wn_raw[:, :, :], w_n.rearrange("t o i -> o t i")).then_inc(got_wn, 16)
            sp.dma_start(nt_raw[0:NT - 1, :], ntype[0:(NT - 1) * P].rearrange("(p c) -> p c", c=P)
                         ).then_inc(got_nt, 16)
            sp.dma_start(nt_raw[NT - 1:NT, 0:TAIL], ntype[(NT - 1) * P:N].rearrange("(p c) -> p c", p=1)
                         ).then_inc(got_nt, 16)

            def store_batch(b, par, tiles=XB, rows=P):
                sp.wait_ge(tab_ready, b + 1)
                dest = table[bass.ds(b * (XB * P * T), tiles * rows * T), :]
                sp.dma_start(dest.rearrange("(j p t) d -> p j (t d)", p=rows, t=T),
                             tab[0:rows, par, 0:tiles, :]).then_inc(tab_stored[par], 16)

            def pair(k):
                for par in range(2):
                    b = 2 * k + par
                    sp.wait_ge(x_turned, b + 1)
                    load_x(b + 2, par)
                    store_batch(b, par)

            def stats_turn():
                sp.wait_ge(stats_set, 1)
                sp.dma_start(stats_dram.rearrange("(p c) -> p c", c=ST), stats[:, :]).then_inc(stats_out, 16)
                sp.wait_ge(stats_out, 16)
                sp.dma_start(row_f[:, :], stats_dram.rearrange("(a c) -> a c", a=1)).then_inc(stats_in, 16)

            pair(0)
            stats_turn()
            with sp.Fori(1, NB // 2 - 1) as k:
                pair(k)
            for par in range(2):
                b = NB - 2 + par
                if par == 0:
                    sp.wait_ge(x_turned, b + 1)
                    sp.dma_start(xin[0:TAIL, par, 0, :], x[(NT - 1) * P:N, :]).then_inc(got_x[par], 16)
                store_batch(b, par)
            store_batch(NB, 0, tiles=1, rows=TAIL)

            def load_fin(j, rows=P):
                sp.dma_start(x_fin[0:rows, :], x[bass.ds(j * P, rows), :]).then_inc(fin_x, 16)

            def store_fin(j, nth, rows=P):
                sp.wait_ge(fin_y, nth + 1)
                sp.dma_start(out[bass.ds(j * P, rows), :], y[0:rows, :]).then_inc(stored, 16)

            def all_fin(start):
                load_fin(0)
                with sp.Fori(0, NT - 2) as j:
                    store_fin(j, j + start)
                    load_fin(j + 1)
                store_fin(NT - 2, NT - 2 + start)
                load_fin(NT - 1, TAIL)
                store_fin(NT - 1, NT - 1 + start, TAIL)

            sp.wait_ge(consts_set, 1)
            all_fin(0)
            sp.wait_ge(stored, NT * 16)
            sp.wait_ge(ctl_set, 1)
            need = sp.value_load(ctl[0:1, 0:1], min_val=0, max_val=1)
            with sp.If(need > 0):
                all_fin(NT)
                sp.wait_ge(stored, 2 * NT * 16)

        @block.gpsimd
        def _(pool):
            pool.memset(dst_raw[:, LAST:ROW], N - 1).then_inc(pads_set, 1)
            pool.memset(src_raw[:, LAST:ROW], -1).then_inc(pads_set, 1)
            pool.memset(typ_raw[:, LAST:ROW], T).then_inc(pads_set, 1)
            pool.memset(nt_raw[:, TAIL:P], 0).then_inc(pads_set, 1)
            pool.memset(ident[:, :], 0.0).then_inc(ident_set, 1)
            pool.wait_ge(ident_set, 1)
            pool.affine_select(out=ident[:, :], in_=ident[:, :], compare_op=ALU.not_equal, fill=1.0, base=0,
                               pattern=[[-1, P]], channel_multiplier=1).then_inc(ident_set, 1)
            pool.iota(limit[:, 0:FIN + 1], pattern=[[0, FIN + 1]], base=-P, channel_multiplier=P,
                      allow_small_or_imprecise_dtypes=True)
            pool.iota(limit[:, FIN + 1:NG], pattern=[[0, NG - FIN - 1]], base=0, channel_multiplier=P,
                      allow_small_or_imprecise_dtypes=True).then_inc(limits_set, 1)
            pool.iota(hot_iota[:, :], pattern=[[TYPE_STEP, T], [1, WIN]], base=0, channel_multiplier=0,
                      allow_small_or_imprecise_dtypes=True).then_inc(hot_iota_set, 1)
            pool.memset(ones[:, :], 1.0)
            pool.memset(eps[:, :], EPS)
            pool.memset(x_fin[:, :], 0.0).then_inc(consts_set, 1)
            pool.wait_ge(got_edges, 6 * 16)
            pool.tensor_scalar(src_raw[:, :], src_raw[:, :], T, None, ALU.mult).then_inc(prep_step, 1)
            pool.wait_ge(prep_step, 1)
            pool.tensor_tensor(src_raw[:, :], src_raw[:, :], typ_raw[:, :], ALU.add).then_inc(prep_step, 1)
            pool.wait_ge(prep_step, 2)
            pool.tensor_copy(idx_f[:, :], src_raw[:, :]).then_inc(keys_set, 1)
            pool.tensor_scalar(typ_raw[:, :], typ_raw[:, :], TYPE_STEP, None, ALU.mult).then_inc(prep_step, 1)
            pool.wait_ge(prep_step, 3)
            pool.tensor_tensor(typ_raw[:, :], typ_raw[:, :], dst_raw[:, :], ALU.add).then_inc(prep_step, 1)
            pool.wait_ge(prep_step, 4)
            pool.wait_ge(minmax_set, NG)
            for g in range(NG):
                span = slice(FIRST[g] * P, (FIRST[g] + SIZES[g]) * P)
                pool.tensor_scalar(key_f[:, span], typ_raw[:, span], stats[:, g:g + 1], None, ALU.subtract
                                   ).then_inc(keys_set, 1)
            for t in range(T):
                pool.memset(acc[:, t, :], 0.0).then_inc(acc_zeroed, 1)

            def gather(slot, signal):
                pool.indirect_dma_start(msg[:, slot, :], None, table,
                                        bass.IndirectOffsetOnAxis(ap=idx_ring[:, slot:slot + 1], axis=0)
                                        ).then_inc(signal, 16)

            def iteration(j, sizes, fixed):
                for g in range(NG):
                    pool.wait_ge(idx_ready, NG * j + g + 1)
                    if not fixed:
                        hold(pool)
                    for c in range(sizes[g]):
                        gather(FIRST[g] + c, gathered[g])

            pool.wait_ge(tab_stored[0], (NB // 2 + 1) * 16)
            pool.wait_ge(tab_stored[1], NB // 2 * 16)
            with pool.Fori(0, NT - 1) as j:
                iteration(j, SIZES, False)
            iteration(NT - 1, LAST_SIZES, True)

            pool.wait_ge(ctl_set, 1)
            need = pool.value_load(ctl[0:1, 0:1], min_val=0, max_val=1)
            with pool.If(need > 0):
                passes = pool.value_load(ctl[0:1, 1:2], min_val=1, max_val=N // WIN + 2)
                with pool.Fori(0, passes) as k:
                    with pool.Fori(0, NT) as j:
                        for g in range(NG):
                            pool.wait_ge(gen_ready, (k * NT + j) * (2 * NG) + 2 * g + 2)
                            hold(pool)
                            for c in range(SIZES[g]):
                                gather(FIRST[g] + c, gen_gathered[g])

        @block.scalar
        def _(act):
            def setup_copy(first, last):
                for u in range(first, last):
                    name, pieces, width = UNITS[u]
                    bank = ps[:, u % SETUP_BANKS, 0:pieces * width]
                    nth = sum(UNITS[i][0] == name for i in range(u))
                    if name == "we":
                        dest = we_t[:, :]
                    elif name == "wn":
                        dest = wn_t[:, nth, :]
                    elif name == "nt":
                        dest = nt_t[:, :]
                    else:
                        whole = key_t if name == "key" else idx_t
                        dest = whole[:, :, :].rearrange("p j c -> p c j")[:, 10 * nth:10 * nth + pieces, :]
                        bank = bank.rearrange("p (c j) -> p c j", j=NT)
                    act.wait_ge(setup_t, u + 1)
                    act.activation(dest, bank, ACT.Copy).then_inc(setup_copied, 1)

            def copy_xt(b, par, first=False):
                act.wait_ge(x_turned, b + 1)
                if not first:
                    act.wait_ge(msg_made, XB * (b - 1))
                act.activation(xt[:, par, :, :], ps[:, XT_PS[par], :].rearrange("p (j n) -> p j n", n=P),
                               ACT.Copy).then_inc(xt_copied, 1)

            def relu_batch(b, par, tiles=XB):
                act.wait_ge(biased, XB * b + tiles)
                act.activation(tab[:, par, 0:tiles, :], tab[:, par, 0:tiles, :], ACT.Relu).then_inc(tab_ready, 1)

            setup_copy(0, 1)
            copy_xt(0, 0, first=True)
            copy_xt(1, 1, first=True)
            relu_batch(0, 0)
            copy_xt(2, 0)
            relu_batch(1, 1)
            setup_copy(1, len(UNITS))
            with act.Fori(1, NB // 2) as k:
                for par in range(2):
                    copy_xt(2 * k + par + 1, 1 - par)
                    relu_batch(2 * k + par, par)
            relu_batch(NB, 0, 1)

            def finish(j, nth, first, added=None):
                act.wait_ge(fin_xt, nth + 1)
                if not first:
                    act.wait_ge(fin_lin, nth)
                act.activation(stage[:, 0, :], ps[:, XPS, 0:P], ACT.Relu).then_inc(stage_xt, 1)
                if added is not None:
                    act.wait_ge(group_added, added)
                hold(act)
                act.activation(stage[:, 1:T + 1, :], acc[:, :, bass.ds(j * P, P)], ACT.Copy).then_inc(stage_acc, 1)
                act.wait_ge(fin_var, nth + 1)
                act.activation(sd[:, :], mv[:, 1:2], ACT.Sqrt, bias=eps[:, :]).then_inc(fin_sd, 1)

            act.wait_ge(consts_set, 1)
            finish(0, 0, True, NG + FIN + 1)
            with act.Fori(1, NT - 2) as j:
                finish(j, j, False, NG * (j + 1) + FIN + 1)
            finish(NT - 2, NT - 2, False, NG * (NT - 1) + FIN + 1)
            finish(NT - 1, NT - 1, False, NG * NT)

            act.wait_ge(ctl_set, 1)
            need = act.value_load(ctl[0:1, 0:1], min_val=0, max_val=1)
            with act.If(need > 0):
                act.wait_ge(gen_done, 1)
                with act.Fori(0, NT) as j:
                    finish(j, j + NT, False)

        @block.vector
        def _(dve):
            steps = [0]

            def link(ins):
                steps[0] += 1
                ins.then_inc(vec_step, 1)
                dve.wait_ge(vec_step, steps[0])

            dve.wait_ge(got_edges, 6 * 16)
            for g in range(NG):
                span = slice(FIRST[g] * P, (FIRST[g] + SIZES[g]) * P)
                dve.tensor_reduce(stats[:, g:g + 1], dst_raw[:, span], AX.X, ALU.min).then_inc(minmax_set, 1)
            for g in range(NG):
                span = slice(FIRST[g] * P, (FIRST[g] + SIZES[g]) * P)
                dve.tensor_reduce(top[:, g:g + 1], dst_raw[:, span], AX.X, ALU.max).then_inc(minmax_set, 1)
            dve.wait_ge(minmax_set, 2 * NG)
            dve.wait_ge(limits_set, 1)
            dve.tensor_tensor(top[:, 0:NG], top[:, 0:NG], stats[:, 0:NG], ALU.subtract)
            link(dve.tensor_tensor(top[:, NG:2 * NG], limit[:, :], stats[:, 0:NG], ALU.subtract))
            dve.tensor_reduce(stats[:, NG:NG + 1], top[:, 0:NG], AX.X, ALU.max)
            dve.tensor_reduce(stats[:, NG + 1:NG + 2], top[:, NG:2 * NG], AX.X, ALU.max).then_inc(stats_set, 1)
            dve.wait_ge(got_nt, 32)
            dve.tensor_copy(nt_f[:, :], nt_raw[:, :]).then_inc(nt_cast, 1)

            def bias_batch(b, par, tiles=XB, first=False, rest=None):
                if not first:
                    dve.wait_ge(tab_stored[par], rest)
                for i in range(tiles):
                    dve.wait_ge(msg_made, XB * b + i + 1)
                    dve.tensor_tensor(tab[:, par, i, :], ps[:, MSG_PS + i, 0:T * D], be_b[:, :], ALU.add
                                      ).then_inc(biased, 1)

            dve.wait_ge(got_bias, 32)
            for par in range(2):
                bias_batch(par, par, first=True)
            with dve.Fori(1, NB // 2) as k:
                for par in range(2):
                    bias_batch(2 * k + par, par, rest=16 * k)
            bias_batch(NB, 0, 1, rest=16 * (NB // 2))

            dve.wait_ge(setup_copied, len(UNITS))
            for t in range(T):
                ins = dve.tensor_scalar(mask[:, t, :], nt_t[:, :], float(t), None, ALU.is_equal)
            ins.then_inc(masks_set, 1)

            def load_rows(j, g, n, signal):
                dve.tensor_copy(idx_ring[:, FIRST[g]:FIRST[g] + n], idx_t[:, j, FIRST[g]:FIRST[g] + n]
                                ).then_inc(signal, 1)

            def one_hot(j, g, n, signal):
                keys = key_t[:, j, FIRST[g]:FIRST[g] + n].rearrange("p (c o) -> p c o", o=1)
                dve.tensor_tensor(hot[:, FIRST[g]:FIRST[g] + n, :], keys.broadcast_to((P, n, T * WIN)),
                                  hot_iota[:, :].rearrange("p (o c) -> p o c", o=1).broadcast_to((P, n, T * WIN)),
                                  ALU.is_equal).then_inc(signal, 1)

            def add_group(g, base, signal):
                cols = acc[:, :, bass.ds(base, WIN)]
                dve.tensor_tensor(cols, ps[:, AGG + g, 0:T * WIN].rearrange("p (t c) -> p t c", t=T), cols,
                                  ALU.add).then_inc(signal, 1)

            def at(j):
                return slice(j, j + 1) if isinstance(j, int) else bass.ds(j, 1)

            dve.wait_ge(hot_iota_set, 1)
            for g in range(NG):
                load_rows(0, g, SIZES[g], idx_ready)
                one_hot(0, g, SIZES[g], hot_ready)

            dve.wait_ge(stats_in, 16)
            rows = row_f[:, :].rearrange("a (j s) -> a s j", s=ST)
            dve.tensor_copy(row_i[:, :], row_f[:, :])
            dve.tensor_reduce(ctl_f[:, 0:1], rows[:, NG, :], AX.X, ALU.max)
            link(dve.tensor_reduce(ctl_f[:, 1:2], rows[:, NG + 1, :], AX.X, ALU.max))
            dve.tensor_scalar(ctl_f[:, 2:3], ctl_f[:, 0:1], float(WIN) - 0.5, None, ALU.is_gt)
            dve.tensor_scalar(ctl_f[:, 3:4], ctl_f[:, 1:2], 0.5, None, ALU.is_gt)
            link(dve.tensor_scalar(ctl_f[:, 4:5], ctl_f[:, 0:1], 1.0 / WIN, 1.0, ALU.mult, ALU.add))
            dve.tensor_tensor(ctl[:, 0:1], ctl_f[:, 2:3], ctl_f[:, 3:4], ALU.max)
            dve.tensor_copy(ctl[:, 1:2], ctl_f[:, 4:5]).then_inc(ctl_set, 1)
            dve.wait_ge(ctl_set, 1)
            dve.wait_ge(acc_zeroed, T)

            def finish(j, nth, first):
                done = [0]

                def fin_link(ins):
                    done[0] += 1
                    ins.then_inc(fin_step, 1)
                    dve.wait_ge(fin_step, nth * FIN_STEPS + done[0])

                dve.wait_ge(fin_x, 16 * (nth + 1))
                dve.wait_ge(fin_lin, nth + 1)
                for t in range(T):
                    fin_link(dve.scalar_tensor_tensor(h[:, :], ps[:, FPS, t * D:(t + 1) * D], mask[:, t, at(j)],
                                                      h[:, :] if t else x_fin[:, :], ALU.mult, ALU.add))
                fin_link(dve.tensor_tensor(h[:, :], h[:, :], x_fin[:, :], ALU.add))
                fin_link(dve.bn_stats(bnst[:, :], h[:, :]))
                hold(dve)
                dve.bn_aggr(mv[:, :], bnst[:, :]).then_inc(fin_var, 1)
                dve.wait_ge(fin_sd, nth + 1)
                fin_link(dve.reciprocal(rstd[:, :], sd[:, :]))
                dve.wait_ge(fin_var, nth + 1)
                if not first:
                    dve.wait_ge(stored, 16 * nth)
                dve.tensor_scalar(y[:, :], h[:, :], mv[:, 0:1], rstd[:, :], ALU.subtract, ALU.mult
                                  ).then_inc(fin_y, 1)
                assert done[0] == FIN_STEPS

            def iteration(j, first=False, last=False, next_sizes=SIZES):
                for g in range(NG):
                    dve.wait_ge(group_summed, NG * j + g + 1)
                    if not last:
                        load_rows(j + 1, g, next_sizes[g], idx_ready)
                        one_hot(j + 1, g, next_sizes[g], hot_ready)
                    base = dve.value_load(row_i[0:1, at(j * ST + g)], min_val=0, max_val=N - 1)
                    if not (first and g == 0):
                        dve.wait_ge(group_added, NG * j + g)
                    if g == FIN + 1 and not first:
                        dve.wait_ge(stage_acc, j)
                    add_group(g, base, group_added)
                if not first:
                    finish(j - 1, j - 1, j - 1 == 0 if isinstance(j, int) else False)

            iteration(0, first=True)
            iteration(1)
            with dve.Fori(2, NT - 2) as j:
                iteration(j)
            iteration(NT - 2, next_sizes=LAST_SIZES)
            iteration(NT - 1, last=True)
            finish(NT - 1, NT - 1, False)

            need = dve.value_load(ctl[0:1, 0:1], min_val=0, max_val=1)
            with dve.If(need > 0):
                passes = dve.value_load(ctl[0:1, 1:2], min_val=1, max_val=N // WIN + 2)
                dve.wait_ge(group_added, NG * NT)
                with dve.Fori(0, passes) as k:
                    dve.tensor_scalar(key_t[:, :, :], key_t[:, :, :], float(-WIN), None, ALU.add
                                      ).then_inc(gen_shift, 1)
                    dve.tensor_scalar(row_f[:, :], row_f[:, :], float(WIN), float(N), ALU.add, ALU.min
                                      ).then_inc(gen_shift, 1)
                    dve.wait_ge(gen_shift, k * SHIFTS + 2)
                    dve.tensor_copy(row_i[:, :], row_f[:, :]).then_inc(gen_shift, 1)
                    dve.wait_ge(gen_shift, k * SHIFTS + 3)
                    hold(dve)
                    with dve.Fori(0, NT) as j:
                        for g in range(NG):
                            nth = (k * NT + j) * NG + g
                            load_rows(j, g, SIZES[g], gen_ready)
                            one_hot(j, g, SIZES[g], gen_ready)
                            dve.wait_ge(gen_summed, nth + 1)
                            base = dve.value_load(row_i[0:1, at(j * ST + g)], min_val=0, max_val=N)
                            add_group(g, base, gen_added)
                            dve.wait_ge(gen_added, nth + 1)
                            hold(dve)
                dve.memset(ctl_f[:, 5:6], 0.0).then_inc(gen_done, 1)
                with dve.Fori(0, NT) as j:
                    finish(j, j + NT, False)

        @block.tensor
        def _(pe):
            def setup_unit(u):
                name, pieces, width = UNITS[u]
                nth = sum(UNITS[i][0] == name for i in range(u))
                if u >= SETUP_BANKS:
                    pe.wait_ge(setup_copied, u - SETUP_BANKS + 1)
                for i in range(pieces):
                    if name == "we":
                        piece = we_raw[:, i, :]
                    elif name == "wn":
                        piece = wn_raw[:, i, nth * D:(nth + 1) * D]
                    elif name == "nt":
                        piece = nt_f[:, :]
                    else:
                        c = 10 * nth + i
                        piece = (key_f if name == "key" else idx_f)[:, c * P:(c + 1) * P]
                    ins = pe.transpose(ps[:, u % SETUP_BANKS, i * width:(i + 1) * width], piece,
                                       ident[0:piece.shape[0], 0:piece.shape[0]])
                ins.then_inc(setup_t, 1)

            def turn_batch(b, par, loads, first=False):
                pe.wait_ge(got_x[par], 16 * loads)
                if not first:
                    pe.wait_ge(xt_copied, b - 1)
                for i in range(XB):
                    ins = pe.transpose(ps[:, XT_PS[par], i * P:(i + 1) * P], xin[:, par, i, :], ident[:, :])
                ins.then_inc(x_turned, 1)

            def make_batch(b, par, tiles=XB, first=False):
                pe.wait_ge(xt_copied, b + 1)
                for i in range(tiles):
                    if not first:
                        pe.wait_ge(biased, XB * (b - 1) + i + 1)
                    pe.matmul(ps[:, MSG_PS + i, 0:T * D], xt[:, par, i, :], we_t[:, :], start=True, stop=True
                              ).then_inc(msg_made, 1)

            pe.wait_ge(ident_set, 2)
            pe.wait_ge(got_we, 16)
            setup_unit(0)
            turn_batch(0, 0, 1, first=True)
            turn_batch(1, 1, 1, first=True)
            pe.wait_ge(setup_copied, 1)
            make_batch(0, 0, first=True)
            turn_batch(2, 0, 2)
            make_batch(1, 1)
            pe.wait_ge(got_wn, 16)
            pe.wait_ge(nt_cast, 1)
            pe.wait_ge(biased, 2 * XB)
            for u in range(1, EDGE_UNIT):
                setup_unit(u)
            pe.wait_ge(keys_set, NG + 1)
            for u in range(EDGE_UNIT, len(UNITS)):
                setup_unit(u)
            pe.wait_ge(setup_copied, len(UNITS))
            with pe.Fori(1, NB // 2) as k:
                for par in range(2):
                    turn_batch(2 * k + par + 1, 1 - par, k + 1 + par)
                    make_batch(2 * k + par, par)
            make_batch(NB, 0, 1)

            def sum_group(g, n, signal):
                for c in range(FIRST[g], FIRST[g] + n):
                    ins = pe.matmul(ps[:, AGG + g, 0:T * WIN], msg[:, c, :], hot[:, c, :],
                                    start=(c == FIRST[g]), stop=(c == FIRST[g] + n - 1))
                ins.then_inc(signal, 1)

            def finish_turn(nth, first):
                pe.wait_ge(fin_x, 16 * (nth + 1))
                if not first:
                    pe.wait_ge(stage_xt, nth)
                pe.transpose(ps[:, XPS, 0:P], x_fin[:, :], ident[:, :]).then_inc(fin_xt, 1)

            def finish_linear(nth, first):
                pe.wait_ge(stage_xt, nth + 1)
                pe.wait_ge(stage_acc, nth + 1)
                if not first:
                    pe.wait_ge(fin_y, nth)
                lin = ps[:, FPS, 0:T * D]
                pe.matmul(lin, ones[:, :], bn_row[:, :], start=True, stop=False)
                for i in range(T + 1):
                    ins = pe.matmul(lin, stage[:, i, :], wn_t[:, i, :], start=False, stop=(i == T))
                ins.then_inc(fin_lin, 1)

            def iteration(j, first=False, sizes=SIZES):
                for g in range(NG):
                    if not first:
                        pe.wait_ge(group_added, NG * (j - 1) + g + 1)
                    pe.wait_ge(hot_ready, NG * j + g + 1)
                    pe.wait_ge(gathered[g], SIZES[g] * 16 * j + sizes[g] * 16)
                    sum_group(g, sizes[g], group_summed)
                    if g == FIN and not first:
                        finish_turn(j - 1, isinstance(j, int) and j == 1)
                    if g == FIN + 1 and not first:
                        finish_linear(j - 1, isinstance(j, int) and j == 1)

            pe.wait_ge(consts_set, 1)
            pe.wait_ge(masks_set, 1)
            pe.wait_ge(biased, XB * NB + 1)
            iteration(0, first=True)
            iteration(1)
            with pe.Fori(2, NT - 1) as j:
                iteration(j)
            iteration(NT - 1, sizes=LAST_SIZES)
            finish_turn(NT - 1, False)
            finish_linear(NT - 1, False)

            pe.wait_ge(ctl_set, 1)
            need = pe.value_load(ctl[0:1, 0:1], min_val=0, max_val=1)
            with pe.If(need > 0):
                passes = pe.value_load(ctl[0:1, 1:2], min_val=1, max_val=N // WIN + 2)
                with pe.Fori(0, passes) as k:
                    with pe.Fori(0, NT) as j:
                        for g in range(NG):
                            pe.wait_ge(gen_ready, (k * NT + j) * (2 * NG) + 2 * g + 2)
                            pe.wait_ge(gen_gathered[g], SIZES[g] * 16 * (k * NT + j + 1))
                            sum_group(g, SIZES[g], gen_summed)
                with pe.Fori(0, NT) as j:
                    finish_turn(j + NT, False)
                    finish_linear(j + NT, False)


_INS = ["x", "src", "dst", "edge_type_3", "node_type_3", "L0_gnn_W_e", "L0_gnn_b_e", "L0_gnn_W_n", "L0_gnn_b_n"]


def kernel(**inputs):
    import numpy as np
    import concourse.bacc as bacc
    from concourse import mybir
    from concourse.bass_utils import run_bass_kernel_spmd

    nc = bacc.Bacc("TRN2", target_bir_lowering=False, num_devices=1)
    arrays, args = {}, []
    for name in _INS:
        a = np.ascontiguousarray(inputs[name])
        arrays[f"in_{name}"] = a
        args.append(nc.dram_tensor(f"in_{name}", a.shape, mybir.dt.from_np(a.dtype), kind="ExternalInput").ap())
    out = nc.dram_tensor("out_0", (6250, 128), mybir.dt.float32, kind="ExternalOutput").ap()
    build(nc, *args, out)
    r = run_bass_kernel_spmd(nc, [arrays], core_ids=[0])
    return r.results[0]["out_0"]
```

```python
from contextlib import ExitStack

import concourse.bass as bass
from concourse import mybir

F32 = mybir.dt.float32
I32 = mybir.dt.int32
ALU = mybir.AluOpType
ACT = mybir.ActivationFunctionType
AX = mybir.AxisListType

P = 128
N, D, T, E = 6250, 128, 3, 106250
EPS = 1e-5

NT = -(-N // P)
TAIL = N - (NT - 1) * P
CT = -(-E // (NT * P))
ROW = CT * P
SIZES = [4, 4, 3, 3, 3]
assert sum(SIZES) == CT
NG = len(SIZES)
FIRST = [sum(SIZES[:g]) for g in range(NG)]
NI = NT - 3
LAST_SIZES = [4, 4, 3, 3, 1]
LAST_COL = sum(LAST_SIZES) * P
MAIN = (NI - 1) * ROW + LAST_COL
EDGE_LOADS = 6 + (ROW - LAST_COL) // P
ET = -(-(E - MAIN) // P)
ELAST = E - MAIN - (ET - 1) * P
PRE = 1
NE = (ET - PRE) // 2
assert PRE + 2 * NE == ET and 2 < NE < NI - 6
FIN = 2
WIN = 42
TYPE_STEP = 16384
assert TYPE_STEP > 2 * N + WIN
ZC = -(-(N + WIN) // 8)
NPAD = 8 * ZC
HALF = 4 * ZC
ST = NG + 3
EST = 3
STATS = NI * ST + ET * EST

NA, NZ = NT - 4, 4
assert NA == NI - 1
ORDER = [NT - 1, NT - 2, NT - 3, NT - 4]
AHEAD = (NT - 3) * P - 1
EARLY_BACK = NE * P

XB = 4
NB = (NT - 1) // XB
assert NB * XB == NT - 1 and NB == 12

AGG = [0, 1, 2, 0, 1]
BEFORE = [3, 4, 2, 0, 1]
LIN_PS, FIN_XT_PS = (3, 6), (4, 5)
E_XT_PS, E_MSG_PS, E_SUM_PS = 5, 6, 7
SETUP_BANKS = (0, 5)
PEELED = 4
MSG_PS, XT_PS = 1, (6, 7)


def build(nc, x, src, dst, etype, ntype, w_e, b_e, w_n, b_n, out):
    table = nc.dram_tensor("message_table", [N * T, D], F32, kind="Internal").ap()
    stats_dram = nc.dram_tensor("stats_row", [STATS], F32, kind="Internal").ap()

    with ExitStack() as ctx:
        def sb(name, shape, dt=F32):
            return ctx.enter_context(nc.sbuf_tensor(name, shape, dt))

        def sem(name):
            return ctx.enter_context(nc.semaphore(name))

        acc = sb("acc", [P, T, NPAD])
        src_raw = sb("src_raw", [NI, ROW], I32)
        dst_raw = sb("dst_raw", [NI, ROW], I32)
        typ_raw = sb("typ_raw", [NI, ROW], I32)
        idx_f = src_raw[:, :].bitcast(F32)
        key_f = typ_raw[:, :].bitcast(F32)
        idx_t = sb("idx_t", [P, NI, CT], I32)
        key_t = sb("key_t", [P, NI, CT])
        idx_ring = sb("idx_ring", [P, CT], I32)
        hot = sb("hot", [P, CT, T * WIN])
        hot_iota = sb("hot_iota", [P, T * WIN])
        stats = sb("stats", [NI, ST])
        neg_base = sb("neg_base", [NI, NG])
        top = sb("top", [NI, NG])
        back = sb("back", [NI, NG])
        limit = sb("limit", [NI, NG])
        esrc_raw = sb("esrc_raw", [ET, P], I32)
        edst_raw = sb("edst_raw", [ET, P], I32)
        etyp_raw = sb("etyp_raw", [ET, P], I32)
        esrc_f = sb("esrc_f", [ET, P])
        eidx_f = sb("eidx_f", [ET, P])
        ekey_f = sb("ekey_f", [ET, P])
        esrc_t = sb("esrc_t", [P, ET], I32)
        eidx_t = sb("eidx_t", [P, ET], I32)
        ekey_t = sb("ekey_t", [P, ET])
        estats = sb("estats", [ET, EST])
        etop = sb("etop", [ET, 1])
        xg = sb("xg", [P, ET, D])
        xs = sb("xs", [P, 2, D])
        xst = sb("xst", [P, 2, P])
        emsg = sb("emsg", [P, 2, T * D])
        ehot = sb("ehot", [P, 2, T * WIN])
        row_f = sb("row_f", [1, STATS])
        row_i = sb("row_i", [1, STATS], I32)
        ctl_f = sb("ctl_f", [1, 10])
        ctl = sb("ctl", [1, 2], I32)
        xin = sb("xin", [P, 2, XB, D])
        xt = sb("xt", [P, 2, XB, P])
        tab = sb("tab", [P, 2, XB, T * D])
        msg = tab[:, :, :, :].rearrange("p a j c -> p (a j c)")[:, 0:CT * D].rearrange("p (c d) -> p c d", d=D)
        we_raw = sb("we_raw", [P, T, D])
        wn_raw = sb("wn_raw", [P, T, (T + 1) * D])
        we_t = sb("we_t", [P, T * D])
        wn_t = sb("wn_t", [P, T + 1, T * D])
        be_b = sb("be_b", [P, T * D])
        bn_row = sb("bn_row", [1, T * D])
        ones = sb("ones", [1, P])
        zero = sb("zero", [P, 1])
        ident = sb("ident", [P, P])
        nt_raw = sb("nt_raw", [NT, P], I32)
        nt_f = sb("nt_f", [NT, P])
        nt_t = sb("nt_t", [P, NT])
        mask = sb("mask", [P, T, NT])
        x_fin = [sb(f"x_fin{z}", [P, D]) for z in range(2)]
        stage = [sb(f"stage{z}", [P, T + 1, P]) for z in range(2)]
        h = [sb(f"h{z}", [P, D]) for z in range(2)]
        y = [sb(f"y{z}", [P, D]) for z in range(2)]
        bnst = [sb(f"bnst{z}", [P, 6]) for z in range(2)]
        mv = [sb(f"mv{z}", [P, 2]) for z in range(2)]
        sd = [sb(f"sd{z}", [P, 1]) for z in range(2)]
        rstd = [sb(f"rstd{z}", [P, 1]) for z in range(2)]
        eps = sb("eps", [P, 1])
        ps = ctx.enter_context(nc.psum_tensor("ps", [P, 8, 512], F32))

        got_esrc, got_early, got_edges = sem("got_esrc"), sem("got_early"), sem("got_edges")
        got_we, got_wn, got_bias, got_nt = sem("got_we"), sem("got_wn"), sem("got_bias"), sem("got_nt")
        got_x = [sem("got_x0"), sem("got_x1")]
        esrc_pad_set = sem("esrc_pad_set")
        pads_set, ident_set, consts_set, zero_set = (sem("pads_set"), sem("ident_set"), sem("consts_set"),
                                                     sem("zero_set"))
        hot_iota_set, acc_zeroed, limits_set = sem("hot_iota_set"), sem("acc_zeroed"), sem("limits_set")
        esrc_cast, early_set, nt_cast, masks_set = (sem("esrc_cast"), sem("early_set"), sem("nt_cast"),
                                                    sem("masks_set"))
        rows_set, bases_set, keys_set = sem("rows_set"), sem("bases_set"), sem("keys_set")
        keys_shifted, stats_set = sem("keys_shifted"), sem("stats_set")
        stats_out, stats_in, ctl_set = sem("stats_out"), sem("stats_in"), sem("ctl_set")
        setup_t, setup_copied = sem("setup_t"), sem("setup_copied")
        vec_step = sem("vec_step")
        x_turned, xt_copied, msg_made = sem("x_turned"), sem("xt_copied"), sem("msg_made")
        biased, tab_ready = sem("biased"), sem("tab_ready")
        tab_stored = [sem("tab_stored0"), sem("tab_stored1")]
        hot_ready, idx_ready = sem("hot_ready"), sem("idx_ready")
        gathered = [sem(f"gathered{g}") for g in range(NG)]
        group_summed, group_added = sem("group_summed"), sem("group_added")
        x_gathered, e_staged, e_turned, e_copied, e_made = (
            sem("x_gathered"), sem("e_staged"), sem("e_turned"), sem("e_copied"), sem("e_made"))
        e_biased, e_ready, e_hot, e_summed, e_added = (
            sem("e_biased"), sem("e_ready"), sem("e_hot"), sem("e_summed"), sem("e_added"))
        def two(name):
            return [sem(name + "0"), sem(name + "1")]

        fin_x, fin_xt, stage_xt, stage_acc, fin_lin = (two("fin_x"), two("fin_xt"), two("stage_xt"),
                                                       two("stage_acc"), two("fin_lin"))
        fin_step, fin_var, fin_sd, fin_y, stored = (two("fin_step"), two("fin_var"), two("fin_sd"),
                                                    two("fin_y"), two("stored"))
        FIN_STEPS = 6
        gen_shift, gen_ready, gen_summed, gen_added, gen_done = (
            sem("gen_shift"), sem("gen_ready"), sem("gen_summed"), sem("gen_added"), sem("gen_done"))
        gen_gathered = [sem(f"gen_gathered{g}") for g in range(NG)]
        gen_gathered_early = sem("gen_gathered_early")
        SHIFTS = 4
        GEN = NI * NG + ET
        MAX_PASSES = N // WIN + 3

        KP = 512 // NI
        UNITS = ([("esrc", 1, ET), ("we", T, P)] + [("wn", T, P)] * (T + 1)
                 + [("nt", 1, NT), ("ekey", 1, ET), ("eidx", 1, ET)]
                 + [("key", KP, NI), ("key", CT - KP, NI), ("idx", KP, NI), ("idx", CT - KP, NI)])
        UNITS_AFTER = [(2, 4), (4, 6), (6, 9), (9, len(UNITS))]

        block = ctx.enter_context(nc.Block())

        def hold(engine):
            engine.nop(nofuse=True)

        def at(j):
            return slice(j, j + 1) if isinstance(j, int) else bass.ds(j, 1)

        def load_x(engine, b, par):
            engine.dma_start(xin[:, par, :, :],
                             x[bass.ds(b * (XB * P), XB * P), :].rearrange("(j p) d -> p j d", p=P)
                             ).then_inc(got_x[par], 16)

        @block.sync
        def _(sp):
            def load_early(raw, dram, signal):
                first = MAIN
                sp.dma_start(raw[0:ET - 1, :], dram[first:first + (ET - 1) * P].rearrange("(p c) -> p c", c=P)
                             ).then_inc(signal, 16)
                sp.dma_start(raw[ET - 1:ET, 0:ELAST], dram[E - ELAST:E].rearrange("(p c) -> p c", p=1)
                             ).then_inc(signal, 16)

            sp.wait_ge(esrc_pad_set, 1)
            load_early(esrc_raw, src, got_esrc)
            load_x(sp, 0, 0)
            load_x(sp, 1, 1)
            sp.wait_ge(pads_set, 5)
            for raw, dram in ((edst_raw, dst), (etyp_raw, etype)):
                load_early(raw, dram, got_early)
            for raw, dram in ((dst_raw, dst), (src_raw, src), (typ_raw, etype)):
                sp.dma_start(raw[0:NI - 1, :], dram[0:(NI - 1) * ROW].rearrange("(p c) -> p c", c=ROW)
                             ).then_inc(got_edges, 16)
                sp.dma_start(raw[NI - 1:NI, 0:LAST_COL], dram[(NI - 1) * ROW:MAIN].rearrange("(p c) -> p c", p=1)
                             ).then_inc(got_edges, 16)
            for c in range(LAST_COL, ROW, P):
                sp.dma_start(dst_raw[NI - 1:NI, c:c + P], dst[MAIN - P:MAIN].rearrange("(p c) -> p c", p=1)
                             ).then_inc(got_edges, 16)
            sp.dma_start(nt_raw[0:NT - 1, :], ntype[0:(NT - 1) * P].rearrange("(p c) -> p c", c=P)
                         ).then_inc(got_nt, 16)
            sp.dma_start(nt_raw[NT - 1:NT, 0:TAIL], ntype[(NT - 1) * P:N].rearrange("(p c) -> p c", p=1)
                         ).then_inc(got_nt, 16)

            def store_batch(b, par, tiles=XB, rows=P):
                sp.wait_ge(tab_ready, b + 1)
                dest = table[bass.ds(b * (XB * P * T), tiles * rows * T), :]
                sp.dma_start(dest.rearrange("(j p t) d -> p j (t d)", p=rows, t=T),
                             tab[0:rows, par, 0:tiles, :]).then_inc(tab_stored[par], 16)

            with sp.Fori(0, NB // 2) as k:
                for par in range(2):
                    store_batch(2 * k + par, par)
            sp.wait_ge(stats_set, 2)
            sp.dma_start(stats_dram[0:NI * ST].rearrange("(p c) -> p c", c=ST), stats[:, :]
                         ).then_inc(stats_out, 16)
            sp.dma_start(stats_dram[NI * ST:STATS].rearrange("(p c) -> p c", c=EST), estats[:, :]
                         ).then_inc(stats_out, 16)
            sp.wait_ge(stats_out, 32)
            sp.dma_start(row_f[:, :], stats_dram.rearrange("(a c) -> a c", a=1)).then_inc(stats_in, 16)
            store_batch(NB, 0, tiles=1, rows=TAIL)

            def load_fin(j, z=0, rows=P):
                sp.dma_start(x_fin[z][0:rows, :], x[bass.ds(j * P, rows), :]).then_inc(fin_x[z], 16)

            def store_fin(j, nth, z=0, rows=P):
                sp.wait_ge(fin_y[z], nth + 1)
                sp.dma_start(out[bass.ds(j * P, rows), :], y[z][0:rows, :]).then_inc(stored[z], 16)

            sp.wait_ge(consts_set, 1)
            load_fin(0)
            load_fin(ORDER[0], 1, TAIL)
            with sp.Fori(0, NE - 1) as j:
                store_fin(j, j)
                load_fin(j + 1)
            for n in range(3):
                store_fin(ORDER[n], n, 1, P if n else TAIL)
                load_fin(ORDER[n + 1], 1)
                store_fin(NE - 1 + n, NE - 1 + n)
                load_fin(NE + n)
            with sp.Fori(NE + 2, NA - 1) as j:
                store_fin(j, j)
                load_fin(j + 1)
            store_fin(NA - 1, NA - 1)
            store_fin(ORDER[3], 3, 1)
            sp.wait_ge(stored[0], NA * 16)
            sp.wait_ge(stored[1], NZ * 16)
            sp.wait_ge(ctl_set, 1)
            need = sp.value_load(ctl[0:1, 0:1], min_val=0, max_val=1)
            with sp.If(need > 0):
                load_fin(0)
                with sp.Fori(0, NT - 2) as j:
                    store_fin(j, j + NA)
                    load_fin(j + 1)
                store_fin(NT - 2, NT - 2 + NA)
                load_fin(NT - 1, 0, TAIL)
                store_fin(NT - 1, NT - 1 + NA, 0, TAIL)
                sp.wait_ge(stored[0], (NA + NT) * 16)

        @block.gpsimd
        def _(pool):
            pool.memset(esrc_raw[:, ELAST:P], 0).then_inc(esrc_pad_set, 1)
            pool.memset(edst_raw[:, ELAST:P], N - 1).then_inc(pads_set, 1)
            pool.memset(etyp_raw[:, ELAST:P], T).then_inc(pads_set, 1)
            pool.memset(nt_raw[:, TAIL:P], 0).then_inc(pads_set, 1)
            pool.memset(src_raw[:, LAST_COL:ROW], 0).then_inc(pads_set, 1)
            pool.memset(typ_raw[:, LAST_COL:ROW], T).then_inc(pads_set, 1)
            pool.memset(ident[:, :], 0.0).then_inc(ident_set, 1)
            pool.memset(zero[:, :], 0.0).then_inc(zero_set, 1)
            pool.wait_ge(ident_set, 1)
            pool.affine_select(out=ident[:, :], in_=ident[:, :], compare_op=ALU.not_equal, fill=1.0, base=0,
                               pattern=[[-1, P]], channel_multiplier=1).then_inc(ident_set, 1)
            pool.iota(limit[:, 0:FIN + 1], pattern=[[0, FIN + 1]], base=-P, channel_multiplier=P,
                      allow_small_or_imprecise_dtypes=True)
            pool.iota(limit[:, FIN + 1:NG], pattern=[[0, NG - FIN - 1]], base=0, channel_multiplier=P,
                      allow_small_or_imprecise_dtypes=True).then_inc(limits_set, 1)
            pool.iota(hot_iota[:, :], pattern=[[TYPE_STEP, T], [1, WIN]], base=0, channel_multiplier=0,
                      allow_small_or_imprecise_dtypes=True).then_inc(hot_iota_set, 1)
            pool.memset(ones[:, :], 1.0)
            pool.memset(x_fin[1][:, :], 0.0)
            pool.memset(eps[:, :], EPS).then_inc(consts_set, 1)
            pool.memset(acc[:, 0, 0:HALF], 0.0).then_inc(acc_zeroed, 1)

            pool.wait_ge(setup_copied, 1)
            for q in range(ET):
                pool.indirect_dma_start(xg[:, q, :], None, x,
                                        bass.IndirectOffsetOnAxis(ap=esrc_t[:, q:q + 1], axis=0)
                                        ).then_inc(x_gathered, 16)

            def gather(slot, signal):
                pool.indirect_dma_start(msg[:, slot, :], None, table,
                                        bass.IndirectOffsetOnAxis(ap=idx_ring[:, slot:slot + 1], axis=0)
                                        ).then_inc(signal, 16)

            pool.wait_ge(tab_stored[0], (NB // 2 + 1) * 16)
            pool.wait_ge(tab_stored[1], NB // 2 * 16)

            def iteration(j, sizes):
                for g in range(NG):
                    pool.wait_ge(idx_ready, NG * j + g + 1)
                    hold(pool)
                    for c in range(sizes[g]):
                        gather(FIRST[g] + c, gathered[g])

            with pool.Fori(0, NI - 1) as j:
                iteration(j, SIZES)
            iteration(NI - 1, LAST_SIZES)

            pool.wait_ge(ctl_set, 1)
            need = pool.value_load(ctl[0:1, 0:1], min_val=0, max_val=1)
            with pool.If(need > 0):
                passes = pool.value_load(ctl[0:1, 1:2], min_val=1, max_val=MAX_PASSES)
                with pool.Fori(0, passes) as k:
                    with pool.Fori(0, NI) as j:
                        for g in range(NG):
                            pool.wait_ge(gen_ready, 2 * (k * GEN + j * NG + g + 1))
                            hold(pool)
                            for c in range(SIZES[g]):
                                gather(FIRST[g] + c, gen_gathered[g])
                    with pool.Fori(0, ET) as q:
                        pool.wait_ge(gen_ready, 2 * (k * GEN + NI * NG + q + 1))
                        hold(pool)
                        gather(0, gen_gathered_early)

        @block.scalar
        def _(act):
            act.dma_start(we_raw[:, :, :], w_e.rearrange("t o i -> o t i")).then_inc(got_we, 16)
            act.dma_start(be_b[:, :], b_e.rearrange("(a t) o -> a (t o)", a=1).broadcast_to((P, T * D))
                          ).then_inc(got_bias, 16)
            act.dma_start(wn_raw[:, :, :], w_n.rearrange("t o i -> o t i")).then_inc(got_wn, 16)
            act.dma_start(bn_row[:, :], b_n.rearrange("(a t) o -> a (t o)", a=1)).then_inc(got_bias, 16)

            def setup_copy(first, last):
                for u in range(first, last):
                    name, pieces, width = UNITS[u]
                    bank = ps[:, SETUP_BANKS[u % 2], 0:pieces * width]
                    nth = sum(UNITS[i][0] == name for i in range(u))
                    if name == "wn":
                        dest = wn_t[:, nth, :]
                    elif name in ("key", "idx"):
                        whole = key_t if name == "key" else idx_t
                        dest = whole[:, :, :].rearrange("p j c -> p c j")[:, KP * nth:KP * nth + pieces, :]
                        bank = bank.rearrange("p (c j) -> p c j", j=NI)
                    else:
                        dest = {"esrc": esrc_t, "we": we_t, "nt": nt_t, "ekey": ekey_t, "eidx": eidx_t}[name][:, :]
                    act.wait_ge(setup_t, u + 1)
                    act.activation(dest, bank, ACT.Copy).then_inc(setup_copied, 1)

            def copy_xt(b, par, first=False, load="batch"):
                act.wait_ge(x_turned, b + 1)
                if load == "batch":
                    if not isinstance(b, int):
                        hold(act)
                    load_x(act, b + 2, par)
                elif load == "tail":
                    act.dma_start(xin[0:TAIL, par, 0, :], x[(NT - 1) * P:N, :]).then_inc(got_x[par], 16)
                if not first:
                    act.wait_ge(msg_made, XB * (b - 1))
                act.activation(xt[:, par, :, :], ps[:, XT_PS[par], :].rearrange("p (j n) -> p j n", n=P),
                               ACT.Copy).then_inc(xt_copied, 1)

            def relu_batch(b, par, tiles=XB):
                act.wait_ge(biased, XB * b + tiles)
                act.activation(tab[:, par, 0:tiles, :], tab[:, par, 0:tiles, :], ACT.Relu).then_inc(tab_ready, 1)

            def zero_acc(part, n):
                act.activation(part, zero[:, 0:1].broadcast_to((P, n)), ACT.Copy).then_inc(acc_zeroed, 1)

            act.wait_ge(zero_set, 1)
            zero_acc(acc[:, 0, HALF:NPAD], HALF)
            setup_copy(0, 2)
            copy_xt(0, 0, first=True)
            copy_xt(1, 1, first=True)
            for b in range(PEELED):
                if b == 3:
                    setup_copy(*UNITS_AFTER[b])
                relu_batch(b, b % 2)
                if b + 2 <= PEELED:
                    copy_xt(b + 2, b % 2)
                if b < 2:
                    zero_acc(acc[:, 1, 2 * b * ZC:2 * (b + 1) * ZC], 2 * ZC)
                if b < 3:
                    setup_copy(*UNITS_AFTER[b])
                if b == 2:
                    act.wait_ge(bases_set, NG + 1)
                    act.wait_ge(keys_set, 1)
                    for g in range(NG):
                        span = slice(FIRST[g] * P, (FIRST[g] + SIZES[g]) * P)
                        act.activation(key_f[:, span], key_f[:, span], ACT.Identity, bias=neg_base[:, g:g + 1]
                                       ).then_inc(keys_shifted, 1)

            def batch(b, par, load="batch"):
                copy_xt(b + 1, 1 - par, load=load)
                relu_batch(b, par)
                zero_acc(acc[:, 2, bass.ds((b - PEELED) * ZC, ZC)], ZC)

            with act.Fori(PEELED // 2, NB // 2 - 2) as k:
                for par in range(2):
                    batch(2 * k + par, par)
            for b in range(NB - 4, NB):
                batch(b, b % 2, load={NB - 4: "batch", NB - 3: "tail"}.get(b))
            relu_batch(NB, 0, 1)

            def early_stage(q, slot, first=False):
                if not first:
                    act.wait_ge(e_turned, q - 1)
                    hold(act)
                act.activation(xs[:, slot, :], xg[:, at(q), :].rearrange("p a d -> p (a d)"), ACT.Copy
                               ).then_inc(e_staged, 1)

            def early_copy(q, slot, first=False):
                if not first:
                    act.wait_ge(e_made, q - 1)
                act.wait_ge(e_turned, q + 1)
                act.activation(xst[:, slot, :], ps[:, E_XT_PS, 0:P], ACT.Copy
                               ).then_inc(e_copied, 1)

            def early_relu(q, slot):
                act.wait_ge(e_biased, q + 1)
                act.activation(emsg[:, slot, :], emsg[:, slot, :], ACT.Relu).then_inc(e_ready, 1)

            def finish_x(nth, z=0, first=False):
                act.wait_ge(fin_xt[z], nth + 1)
                if not first:
                    act.wait_ge(fin_lin[z], nth)
                act.activation(stage[z][:, 0, :], ps[:, FIN_XT_PS[z], 0:P], ACT.Relu).then_inc(stage_xt[z], 1)

            def finish_acc(tile, z=0, added=None):
                if added is not None:
                    act.wait_ge(group_added, added)
                    hold(act)
                act.activation(stage[z][:, 1:T + 1, :], acc[:, :, bass.ds(tile * P, P)], ACT.Copy
                               ).then_inc(stage_acc[z], 1)

            def finish_sd(nth, z=0):
                act.wait_ge(fin_var[z], nth + 1)
                act.activation(sd[z][:, :], mv[z][:, 1:2], ACT.Sqrt, bias=eps[:, :]).then_inc(fin_sd[z], 1)

            def iteration(j, early=False, fin=True, extra=None, last=False):
                q = PRE + 2 * j
                if extra is not None:
                    finish_x(extra, 1, first=extra == 0)
                    finish_acc(ORDER[extra], 1, NG * j + 1)
                    finish_sd(extra, 1)
                if early:
                    early_stage(q, 1)
                    early_copy(q, 1)
                    early_relu(q, 1)
                    early_stage(q + 1, 0)
                    early_copy(q + 1, 0)
                if fin:
                    finish_x(j - 1, first=isinstance(j, int) and j == 1)
                    finish_acc(j - 1, added=NG * j + FIN + 1)
                if early:
                    early_relu(q + 1, 0)
                if last:
                    finish_x(3, 1)
                    finish_acc(ORDER[3], 1, NG * NI)
                if fin:
                    finish_sd(j - 1)
                if last:
                    finish_sd(3, 1)

            act.wait_ge(x_gathered, 16 * ET)
            act.wait_ge(consts_set, 1)
            for q in range(PRE):
                early_stage(q, q % 2, first=q < 2)
                early_copy(q, q % 2, first=q < 2)
                early_relu(q, q % 2)
            iteration(0, True, False)
            iteration(1, True)
            with act.Fori(2, NE) as j:
                iteration(j, True)
            for n in range(3):
                iteration(NE + n, extra=n)
            with act.Fori(NE + 3, NI - 1) as j:
                iteration(j)
            iteration(NI - 1, last=True)

            act.wait_ge(ctl_set, 1)
            need = act.value_load(ctl[0:1, 0:1], min_val=0, max_val=1)
            with act.If(need > 0):
                act.wait_ge(gen_done, 1)
                with act.Fori(0, NT) as j:
                    finish_x(j + NA)
                    finish_acc(j)
                    finish_sd(j + NA)

        @block.vector
        def _(dve):
            steps = [0]

            def link(ins):
                steps[0] += 1
                ins.then_inc(vec_step, 1)
                dve.wait_ge(vec_step, steps[0])

            dve.memset(acc[:, 1, HALF:NPAD], 0.0).then_inc(acc_zeroed, 1)
            dve.wait_ge(got_esrc, 32)
            dve.tensor_copy(esrc_f[:, :], esrc_raw[:, :]).then_inc(esrc_cast, 1)

            def early_prep():
                dve.wait_ge(got_early, 64)
                dve.wait_ge(esrc_cast, 1)
                dve.tensor_reduce(estats[:, 0:1], edst_raw[:, :], AX.X, ALU.min)
                dve.tensor_reduce(etop[:, :], edst_raw[:, :], AX.X, ALU.max)
                dve.scalar_tensor_tensor(ekey_f[:, :], etyp_raw[:, :], float(TYPE_STEP), edst_raw[:, :],
                                         ALU.mult, ALU.add)
                link(dve.scalar_tensor_tensor(eidx_f[:, :], esrc_f[:, :], float(T), etyp_raw[:, :],
                                              ALU.mult, ALU.add))
                dve.tensor_scalar(eidx_f[:, :], eidx_f[:, :], float(N * T - 1), None, ALU.min)
                dve.tensor_tensor(estats[:, 1:2], etop[:, :], estats[:, 0:1], ALU.subtract)
                dve.tensor_scalar(estats[:, 2:3], estats[:, 0:1], -1.0, float(EARLY_BACK), ALU.mult, ALU.add
                                  ).then_inc(stats_set, 1)
                dve.tensor_scalar(ekey_f[:, :], ekey_f[:, :], estats[:, 0:1], None, ALU.subtract
                                  ).then_inc(early_set, 1)

            def spans(signal, out, op):
                for g in range(NG):
                    span = slice(FIRST[g] * P, (FIRST[g] + SIZES[g]) * P)
                    dve.tensor_reduce(out[:, g:g + 1], dst_raw[:, span], AX.X, op).then_inc(signal, 1)

            def bases():
                dve.wait_ge(got_edges, 16 * EDGE_LOADS)
                spans(bases_set, stats, ALU.min)
                dve.wait_ge(bases_set, NG)
                dve.tensor_scalar(neg_base[:, :], stats[:, 0:NG], -1.0, None, ALU.mult).then_inc(bases_set, 1)

            def table_rows():
                dve.scalar_tensor_tensor(idx_f, src_raw[:, :], float(T), typ_raw[:, :], ALU.mult, ALU.add
                                         ).then_inc(rows_set, 1)

            def keys():
                dve.wait_ge(rows_set, 1)
                dve.scalar_tensor_tensor(key_f, typ_raw[:, :], float(TYPE_STEP), dst_raw[:, :], ALU.mult, ALU.add
                                         ).then_inc(keys_set, 1)

            def reach():
                spans(vec_step, top, ALU.max)
                steps[0] += NG
                dve.wait_ge(vec_step, steps[0])
                dve.wait_ge(limits_set, 1)
                dve.tensor_reduce(stats[:, NG + 2:NG + 3], top[:, :], AX.X, ALU.max)
                dve.tensor_tensor(back[:, :], limit[:, :], stats[:, 0:NG], ALU.subtract)
                link(dve.tensor_tensor(neg_base[:, :], top[:, :], stats[:, 0:NG], ALU.subtract))
                dve.tensor_scalar(stats[:, NG + 2:NG + 3], stats[:, NG + 2:NG + 3], float(AHEAD), None, ALU.subtract)
                dve.tensor_reduce(stats[:, NG:NG + 1], neg_base[:, :], AX.X, ALU.max)
                dve.tensor_reduce(stats[:, NG + 1:NG + 2], back[:, :], AX.X, ALU.max).then_inc(stats_set, 1)

            def bias_batch(b, par, tiles=XB, rest=None):
                if rest is not None:
                    dve.wait_ge(tab_stored[par], rest)
                for i in range(tiles):
                    dve.wait_ge(msg_made, XB * b + i + 1)
                    dve.tensor_tensor(tab[:, par, i, :], ps[:, MSG_PS + i, 0:T * D], be_b[:, :], ALU.add
                                      ).then_inc(biased, 1)

            early_prep()
            dve.wait_ge(got_nt, 32)
            dve.tensor_copy(nt_f[:, :], nt_raw[:, :]).then_inc(nt_cast, 1)
            dve.wait_ge(got_bias, 32)
            bias_batch(0, 0)
            bases()
            table_rows()
            bias_batch(1, 1)
            keys()
            bias_batch(2, 0, rest=16)
            bias_batch(3, 1, rest=16)
            dve.wait_ge(keys_shifted, NG)
            reach()
            def load_rows(j, g, n, signal):
                dve.tensor_copy(idx_ring[:, FIRST[g]:FIRST[g] + n], idx_t[:, j, FIRST[g]:FIRST[g] + n]
                                ).then_inc(signal, 1)

            dve.wait_ge(setup_copied, len(UNITS))
            for g in range(NG):
                load_rows(0, g, SIZES[g], idx_ready)
            with dve.Fori(PEELED // 2, NB // 2) as k:
                for par in range(2):
                    bias_batch(2 * k + par, par, rest=16 * k)
            bias_batch(NB, 0, 1, rest=16 * (NB // 2))

            for t in range(T):
                ins = dve.tensor_scalar(mask[:, t, :], nt_t[:, :], float(t), None, ALU.is_equal)
            ins.then_inc(masks_set, 1)

            def one_hot(j, g, n, signal):
                keys = key_t[:, j, FIRST[g]:FIRST[g] + n].rearrange("p (c o) -> p c o", o=1)
                dve.tensor_tensor(hot[:, FIRST[g]:FIRST[g] + n, :], keys.broadcast_to((P, n, T * WIN)),
                                  hot_iota[:, :].rearrange("p (o c) -> p o c", o=1).broadcast_to((P, n, T * WIN)),
                                  ALU.is_equal).then_inc(signal, 1)

            def add_sums(bank, base, signal):
                cols = acc[:, :, bass.ds(base, WIN)]
                dve.tensor_tensor(cols, bank.rearrange("p (t c) -> p t c", t=T), cols, ALU.add).then_inc(signal, 1)

            def group_bank(g):
                return ps[:, AGG[g], 0:T * WIN]

            early_bank = ps[:, E_SUM_PS, 0:T * WIN]

            dve.wait_ge(hot_iota_set, 1)
            for g in range(NG):
                one_hot(0, g, SIZES[g], hot_ready)

            dve.wait_ge(stats_in, 16)
            rows = row_f[:, 0:NI * ST].rearrange("a (j s) -> a s j", s=ST)
            erows = row_f[:, NI * ST:STATS].rearrange("a (j s) -> a s j", s=EST)
            dve.tensor_copy(row_i[:, :], row_f[:, :])
            for s in range(3):
                dve.tensor_reduce(ctl_f[:, s:s + 1], rows[:, NG + s, :], AX.X, ALU.max)
            dve.tensor_reduce(ctl_f[:, 3:4], erows[:, 1, :], AX.X, ALU.max)
            link(dve.tensor_reduce(ctl_f[:, 4:5], erows[:, 2, :], AX.X, ALU.max))
            dve.tensor_tensor(ctl_f[:, 5:6], ctl_f[:, 0:1], ctl_f[:, 3:4], ALU.max)
            dve.tensor_tensor(ctl_f[:, 6:7], ctl_f[:, 1:2], ctl_f[:, 4:5], ALU.max)
            link(dve.tensor_scalar(ctl_f[:, 7:8], ctl_f[:, 2:3], 0.5, None, ALU.is_gt))
            dve.tensor_scalar(ctl_f[:, 8:9], ctl_f[:, 5:6], float(WIN) - 0.5, None, ALU.is_gt)
            dve.tensor_scalar(ctl_f[:, 9:10], ctl_f[:, 6:7], 0.5, None, ALU.is_gt)
            link(dve.tensor_scalar(ctl_f[:, 5:6], ctl_f[:, 5:6], 1.0 / WIN, 1.0, ALU.mult, ALU.add))
            link(dve.tensor_tensor(ctl_f[:, 8:9], ctl_f[:, 8:9], ctl_f[:, 9:10], ALU.max))
            dve.tensor_tensor(ctl[:, 0:1], ctl_f[:, 7:8], ctl_f[:, 8:9], ALU.max)
            link(dve.tensor_copy(ctl[:, 1:2], ctl_f[:, 5:6]))
            dve.nop().then_inc(ctl_set, 1)
            dve.wait_ge(acc_zeroed, 1 + 1 + 1 + 2 + 8)

            def early_hot(q, slot, first=False):
                if not first:
                    dve.wait_ge(e_summed, q - 1)
                dve.tensor_scalar(ehot[:, slot, :], hot_iota[:, :], ekey_t[:, at(q)], None, ALU.is_equal
                                  ).then_inc(e_hot, 1)

            def early_bias(q, slot):
                dve.wait_ge(e_made, q + 1)
                dve.tensor_tensor(emsg[:, slot, :], ps[:, E_MSG_PS, 0:T * D], be_b[:, :], ALU.add
                                  ).then_inc(e_biased, 1)

            def early_base(q):
                return dve.value_load(row_i[0:1, at(NI * ST + EST * q)], min_val=0, max_val=N - 1)

            def early_add(q, groups=None):
                dve.wait_ge(e_summed, q + 1)
                base = early_base(q)
                if groups is not None:
                    dve.wait_ge(group_added, groups)
                elif q:
                    dve.wait_ge(e_added, q)
                add_sums(early_bank, base, e_added)

            def finish(tile, nth, z=0, first=False):
                done = [0]

                def fin_link(ins):
                    done[0] += 1
                    ins.then_inc(fin_step[z], 1)
                    dve.wait_ge(fin_step[z], nth * FIN_STEPS + done[0])

                dve.wait_ge(fin_x[z], 16 * (nth + 1))
                dve.wait_ge(fin_lin[z], nth + 1)
                for t in range(T):
                    fin_link(dve.scalar_tensor_tensor(h[z][:, :], ps[:, LIN_PS[z], t * D:(t + 1) * D], mask[:, t, at(tile)],
                                                      h[z][:, :] if t else x_fin[z][:, :], ALU.mult, ALU.add))
                fin_link(dve.tensor_tensor(h[z][:, :], h[z][:, :], x_fin[z][:, :], ALU.add))
                fin_link(dve.bn_stats(bnst[z][:, :], h[z][:, :]))
                hold(dve)
                dve.bn_aggr(mv[z][:, :], bnst[z][:, :]).then_inc(fin_var[z], 1)
                dve.wait_ge(fin_sd[z], nth + 1)
                fin_link(dve.reciprocal(rstd[z][:, :], sd[z][:, :]))
                dve.wait_ge(fin_var[z], nth + 1)
                if not first:
                    dve.wait_ge(stored[z], 16 * nth)
                dve.tensor_scalar(y[z][:, :], h[z][:, :], mv[z][:, 0:1], rstd[z][:, :], ALU.subtract, ALU.mult
                                  ).then_inc(fin_y[z], 1)
                assert done[0] == FIN_STEPS

            def iteration(j, early=False, fin=True, extra=None, first_plain=False, next_sizes=SIZES):
                q = PRE + 2 * j
                if early:
                    early_hot(q, 1)
                    early_hot(q + 1, 0)
                for g in range(NG):
                    dve.wait_ge(group_summed, NG * j + g + 1)
                    if next_sizes:
                        load_rows(j + 1, g, next_sizes[g], idx_ready)
                        one_hot(j + 1, g, next_sizes[g], hot_ready)
                    base = dve.value_load(row_i[0:1, at(j * ST + g)], min_val=0, max_val=N - 1)
                    if g in (FIN + 1, 0) and early:
                        dve.wait_ge(e_added, q + 1 if g else q)
                    elif g == 0 and first_plain:
                        dve.wait_ge(e_added, ET)
                        dve.wait_ge(group_added, NG * j + g)
                    else:
                        dve.wait_ge(group_added, NG * j + g)
                    if g == FIN + 1 and fin:
                        dve.wait_ge(stage_acc[0], j)
                    if g == 1 and extra is not None:
                        dve.wait_ge(stage_acc[1], extra + 1)
                    add_sums(group_bank(g), base, group_added)
                    if early and g == 1:
                        early_bias(q, 1)
                    if early and g == FIN:
                        early_add(q, NG * j + g + 1)
                    if early and g == FIN + 1:
                        early_bias(q + 1, 0)
                    if extra is not None and g == FIN:
                        finish(ORDER[extra], extra, 1, first=extra == 0)
                if early:
                    early_add(q + 1, NG * (j + 1))
                if fin:
                    finish(j - 1, j - 1, first=isinstance(j, int) and j == 1)

            for q in range(PRE):
                early_hot(q, q % 2, first=q < 2)
                early_bias(q, q % 2)
                early_add(q)
            iteration(0, True, False)
            iteration(1, True)
            with dve.Fori(2, NE) as j:
                iteration(j, True)
            for n in range(3):
                iteration(NE + n, extra=n, first_plain=n == 0)
            with dve.Fori(NE + 3, NI - 2) as j:
                iteration(j)
            iteration(NI - 2, next_sizes=LAST_SIZES)
            iteration(NI - 1, next_sizes=None)
            finish(ORDER[3], 3, 1)

            need = dve.value_load(ctl[0:1, 0:1], min_val=0, max_val=1)
            with dve.If(need > 0):
                passes = dve.value_load(ctl[0:1, 1:2], min_val=1, max_val=MAX_PASSES)
                dve.wait_ge(group_added, NG * NI)
                with dve.Fori(0, passes) as k:
                    dve.tensor_scalar(key_t[:, :, :], key_t[:, :, :], float(-WIN), None, ALU.add
                                      ).then_inc(gen_shift, 1)
                    dve.tensor_scalar(ekey_t[:, :], ekey_t[:, :], float(-WIN), None, ALU.add
                                      ).then_inc(gen_shift, 1)
                    dve.tensor_scalar(row_f[:, :], row_f[:, :], float(WIN), float(N), ALU.add, ALU.min
                                      ).then_inc(gen_shift, 1)
                    dve.wait_ge(gen_shift, k * SHIFTS + 3)
                    dve.tensor_copy(row_i[:, :], row_f[:, :]).then_inc(gen_shift, 1)
                    dve.wait_ge(gen_shift, k * SHIFTS + 4)
                    hold(dve)
                    with dve.Fori(0, NI) as j:
                        for g in range(NG):
                            nth = k * GEN + j * NG + g
                            load_rows(j, g, SIZES[g], gen_ready)
                            one_hot(j, g, SIZES[g], gen_ready)
                            dve.wait_ge(gen_summed, nth + 1)
                            base = dve.value_load(row_i[0:1, at(j * ST + g)], min_val=0, max_val=N)
                            add_sums(group_bank(g), base, gen_added)
                            dve.wait_ge(gen_added, nth + 1)
                            hold(dve)
                    with dve.Fori(0, ET) as q:
                        nth = k * GEN + NI * NG + q
                        dve.tensor_copy(idx_ring[:, 0:1], eidx_t[:, at(q)]).then_inc(gen_ready, 1)
                        dve.tensor_scalar(hot[:, 0, :], hot_iota[:, :], ekey_t[:, at(q)], None, ALU.is_equal
                                          ).then_inc(gen_ready, 1)
                        dve.wait_ge(gen_summed, nth + 1)
                        base = dve.value_load(row_i[0:1, at(NI * ST + EST * q)], min_val=0, max_val=N)
                        add_sums(group_bank(0), base, gen_added)
                        dve.wait_ge(gen_added, nth + 1)
                        hold(dve)
                dve.memset(ctl_f[:, 9:10], 0.0).then_inc(gen_done, 1)
                with dve.Fori(0, NT) as j:
                    finish(j, j + NA)

        @block.tensor
        def _(pe):
            def setup_unit(first, last):
                for u in range(first, last):
                    name, pieces, width = UNITS[u]
                    nth = sum(UNITS[i][0] == name for i in range(u))
                    if u >= len(SETUP_BANKS):
                        pe.wait_ge(setup_copied, u - len(SETUP_BANKS) + 1)
                    for i in range(pieces):
                        if name == "we":
                            piece = we_raw[:, i, :]
                        elif name == "wn":
                            piece = wn_raw[:, i, nth * D:(nth + 1) * D]
                        elif name in ("key", "idx"):
                            c = KP * nth + i
                            piece = (key_f if name == "key" else idx_f)[:, c * P:(c + 1) * P]
                        else:
                            piece = {"esrc": esrc_f, "nt": nt_f, "ekey": ekey_f, "eidx": eidx_f}[name][:, :]
                        ins = pe.transpose(ps[:, SETUP_BANKS[u % 2], i * width:(i + 1) * width], piece,
                                           ident[0:piece.shape[0], 0:piece.shape[0]])
                    ins.then_inc(setup_t, 1)

            def turn_batch(b, par, loads, first=False):
                pe.wait_ge(got_x[par], 16 * loads)
                if not first:
                    pe.wait_ge(xt_copied, b - 1)
                for i in range(XB):
                    ins = pe.transpose(ps[:, XT_PS[par], i * P:(i + 1) * P], xin[:, par, i, :], ident[:, :])
                ins.then_inc(x_turned, 1)

            def make_batch(b, par, tiles=XB, first=False):
                pe.wait_ge(xt_copied, b + 1)
                for i in range(tiles):
                    if not first:
                        pe.wait_ge(biased, XB * (b - 1) + i + 1)
                    pe.matmul(ps[:, MSG_PS + i, 0:T * D], xt[:, par, i, :], we_t[:, :], start=True, stop=True
                              ).then_inc(msg_made, 1)

            pe.wait_ge(ident_set, 2)
            pe.wait_ge(esrc_cast, 1)
            setup_unit(0, 1)
            pe.wait_ge(got_we, 16)
            setup_unit(1, 2)
            turn_batch(0, 0, 1, first=True)
            turn_batch(1, 1, 1, first=True)
            pe.wait_ge(setup_copied, 2)
            for b in range(PEELED):
                make_batch(b, b % 2, first=b == 0)
                if b + 2 <= PEELED:
                    turn_batch(b + 2, b % 2, b // 2 + 2)
                if b == 0:
                    pe.wait_ge(got_wn, 16)
                if b == 2:
                    pe.wait_ge(nt_cast, 1)
                    pe.wait_ge(early_set, 1)
                if b == 3:
                    pe.wait_ge(keys_shifted, NG)
                setup_unit(*UNITS_AFTER[b])
            with pe.Fori(PEELED // 2, NB // 2) as k:
                for par in range(2):
                    turn_batch(2 * k + par + 1, 1 - par, k + 1 + par)
                    make_batch(2 * k + par, par)
            make_batch(NB, 0, 1)

            def early_turn(q, slot, first=False):
                pe.wait_ge(e_staged, q + 1)
                if not first:
                    pe.wait_ge(e_copied, q)
                pe.transpose(ps[:, E_XT_PS, 0:P], xs[:, slot, :], ident[:, :]
                             ).then_inc(e_turned, 1)

            def early_make(q, slot, first=False):
                pe.wait_ge(e_copied, q + 1)
                if not first:
                    pe.wait_ge(e_biased, q)
                pe.matmul(ps[:, E_MSG_PS, 0:T * D], xst[:, slot, :], we_t[:, :], start=True, stop=True
                          ).then_inc(e_made, 1)

            def early_sum(q, slot, first=False):
                pe.wait_ge(e_ready, q + 1)
                pe.wait_ge(e_hot, q + 1)
                if not first:
                    pe.wait_ge(e_added, q)
                for t in range(T):
                    ins = pe.matmul(ps[:, E_SUM_PS, t * WIN:(t + 1) * WIN],
                                    emsg[:, slot, t * D:(t + 1) * D], ehot[:, slot, t * WIN:(t + 1) * WIN],
                                    start=True, stop=True)
                ins.then_inc(e_summed, 1)

            def sum_group(g, n, signal):
                for c in range(FIRST[g], FIRST[g] + n):
                    ins = pe.matmul(ps[:, AGG[g], 0:T * WIN], msg[:, c, :], hot[:, c, :],
                                    start=(c == FIRST[g]), stop=(c == FIRST[g] + n - 1))
                ins.then_inc(signal, 1)

            def finish_turn(nth, z=0, first=False):
                pe.wait_ge(fin_x[z], 16 * (nth + 1))
                if not first:
                    pe.wait_ge(stage_xt[z], nth)
                pe.transpose(ps[:, FIN_XT_PS[z], 0:P], x_fin[z][:, :], ident[:, :]).then_inc(fin_xt[z], 1)

            def linear_open(nth, z=0, first=False):
                lin = ps[:, LIN_PS[z], 0:T * D]
                pe.wait_ge(stage_xt[z], nth + 1)
                if not first:
                    pe.wait_ge(fin_y[z], nth)
                pe.matmul(lin, ones[:, :], bn_row[:, :], start=True, stop=False)
                pe.matmul(lin, stage[z][:, 0, :], wn_t[:, 0, :], start=False, stop=False)

            def linear_close(nth, z=0):
                lin = ps[:, LIN_PS[z], 0:T * D]
                pe.wait_ge(stage_acc[z], nth + 1)
                for i in range(1, T + 1):
                    ins = pe.matmul(lin, stage[z][:, i, :], wn_t[:, i, :], start=False, stop=(i == T))
                ins.then_inc(fin_lin[z], 1)

            def finish_linear(nth, z=0, first=False):
                linear_open(nth, z, first)
                linear_close(nth, z)

            def iteration(j, early=False, fin=True, extra=None, last=False):
                sizes = LAST_SIZES if last else SIZES
                q = PRE + 2 * j
                start = isinstance(j, int) and j == 1
                for g in range(NG):
                    if g > 2 or not (isinstance(j, int) and j == 0):
                        pe.wait_ge(group_added, NG * (j if g > 2 else j - 1) + BEFORE[g] + 1)
                    pe.wait_ge(hot_ready, NG * j + g + 1)
                    pe.wait_ge(gathered[g], SIZES[g] * 16 * j + sizes[g] * 16)
                    sum_group(g, sizes[g], group_summed)
                    if g == 0:
                        if early:
                            early_turn(q, 1)
                        if extra is not None:
                            finish_turn(extra, 1, extra == 0)
                    if g == 1:
                        if early:
                            early_make(q, 1)
                        if extra is not None:
                            finish_linear(extra, 1, extra == 0)
                    if g == FIN:
                        if early:
                            early_sum(q, 1)
                            early_turn(q + 1, 0)
                        if fin:
                            finish_turn(j - 1, first=start)
                        if last:
                            finish_turn(3, 1)
                    if g == FIN + 1:
                        if early:
                            early_make(q + 1, 0)
                        if fin:
                            finish_linear(j - 1, first=start)
                        if last:
                            linear_open(3, 1)
                if early:
                    early_sum(q + 1, 0)

            pe.wait_ge(consts_set, 1)
            pe.wait_ge(masks_set, 1)
            pe.wait_ge(biased, XB * NB + 1)
            for q in range(PRE):
                early_turn(q, q % 2, first=q == 0)
                early_make(q, q % 2, first=q == 0)
                early_sum(q, q % 2, first=q == 0)
            iteration(0, True, False)
            iteration(1, True)
            with pe.Fori(2, NE) as j:
                iteration(j, True)
            for n in range(3):
                iteration(NE + n, extra=n)
            with pe.Fori(NE + 3, NI - 1) as j:
                iteration(j)
            iteration(NI - 1, last=True)
            linear_close(3, 1)

            pe.wait_ge(ctl_set, 1)
            need = pe.value_load(ctl[0:1, 0:1], min_val=0, max_val=1)
            with pe.If(need > 0):
                passes = pe.value_load(ctl[0:1, 1:2], min_val=1, max_val=MAX_PASSES)
                with pe.Fori(0, passes) as k:
                    with pe.Fori(0, NI) as j:
                        for g in range(NG):
                            pe.wait_ge(gen_ready, 2 * (k * GEN + j * NG + g + 1))
                            pe.wait_ge(gen_gathered[g], SIZES[g] * 16 * (k * NI + j + 1))
                            sum_group(g, SIZES[g], gen_summed)
                    with pe.Fori(0, ET) as q:
                        pe.wait_ge(gen_ready, 2 * (k * GEN + NI * NG + q + 1))
                        pe.wait_ge(gen_gathered_early, 16 * (k * ET + q + 1))
                        sum_group(0, 1, gen_summed)
                with pe.Fori(0, NT) as j:
                    finish_turn(j + NA)
                    finish_linear(j + NA)


_INS = ["x", "src", "dst", "edge_type_3", "node_type_3", "L0_gnn_W_e", "L0_gnn_b_e", "L0_gnn_W_n", "L0_gnn_b_n"]


def kernel(**inputs):
    import numpy as np
    import concourse.bacc as bacc
    from concourse import mybir
    from concourse.bass_utils import run_bass_kernel_spmd

    nc = bacc.Bacc("TRN2", target_bir_lowering=False, num_devices=1)
    arrays, args = {}, []
    for name in _INS:
        a = np.ascontiguousarray(inputs[name])
        arrays[f"in_{name}"] = a
        args.append(nc.dram_tensor(f"in_{name}", a.shape, mybir.dt.from_np(a.dtype), kind="ExternalInput").ap())
    out = nc.dram_tensor("out_0", (6250, 128), mybir.dt.float32, kind="ExternalOutput").ap()
    build(nc, *args, out)
    r = run_bass_kernel_spmd(nc, [arrays], core_ids=[0])
    return r.results[0]["out_0"]
```

```python
from contextlib import ExitStack

import concourse.bass as bass
from concourse import mybir

F32 = mybir.dt.float32
I32 = mybir.dt.int32
ALU = mybir.AluOpType
ACT = mybir.ActivationFunctionType
AX = mybir.AxisListType

P = 128
N, D, T, E = 6250, 128, 3, 106250
EPS = 1e-5

NT = -(-N // P)
TAIL = N - (NT - 1) * P
CT = -(-E // (NT * P))
ROW = CT * P
SIZES = [4, 4, 3, 3, 3]
assert sum(SIZES) == CT
NG = len(SIZES)
FIRST = [sum(SIZES[:g]) for g in range(NG)]
KE = 4
NI = NT - KE
LAST_SIZES = [4, 4, 3, 3, 1]
LAST_COL = sum(LAST_SIZES) * P
MAIN = (NI - 1) * ROW + LAST_COL
EDGE_LOADS = 6 + (ROW - LAST_COL) // P
ET = -(-(E - MAIN) // P)
ELAST = E - MAIN - (ET - 1) * P
PRE = 2
NE = (ET - PRE) // 2
SLOTS = (PRE % 2, 1 - PRE % 2)
assert PRE + 2 * NE == ET and 2 < NE < NI - KE - 3
FIN = 2
WIN = 42
TYPE_STEP = 16384
assert TYPE_STEP > 2 * N + WIN
ZC = -(-(N + WIN) // 8)
NPAD = 8 * ZC
HALF = 4 * ZC
ST = NG + 3
EST = 3
STATS = NI * ST + ET * EST

NA, NZ = NI - 1, KE + 1
ORDER = [NT - 1 - n for n in range(NZ)]
AHEAD = NI * P - 1
EARLY_BACK = NE * P

XB = 4
XH = XB // 2
NB = (NT - 1) // XB
assert NB * XB == NT - 1 and NB == 12

AGG = [0, 1, 2, 0, 1]
BEFORE = [3, 4, 2, 0, 1]
LIN_PS, FIN_XT_PS = (3, 6), (4, 5)
E_XT_PS, E_MSG_PS, E_SUM_PS = 5, 6, 7
SETUP_BANKS = (0, 5)
PEELED = 4
MSG_PS, XT_PS = 1, (6, 7)


def build(nc, x, src, dst, etype, ntype, w_e, b_e, w_n, b_n, out):
    table = nc.dram_tensor("message_table", [N * T, D], F32, kind="Internal").ap()
    stats_dram = nc.dram_tensor("stats_row", [STATS], F32, kind="Internal").ap()

    with ExitStack() as ctx:
        def sb(name, shape, dt=F32):
            return ctx.enter_context(nc.sbuf_tensor(name, shape, dt))

        def sem(name):
            return ctx.enter_context(nc.semaphore(name))

        acc = sb("acc", [P, T, NPAD])
        src_raw = sb("src_raw", [NI, ROW], I32)
        dst_raw = sb("dst_raw", [NI, ROW], I32)
        typ_raw = sb("typ_raw", [NI, ROW], I32)
        idx_f = src_raw[:, :].bitcast(F32)
        key_f = typ_raw[:, :].bitcast(F32)
        idx_t = sb("idx_t", [P, NI, CT], I32)
        key_t = sb("key_t", [P, NI, CT])
        idx_ring = sb("idx_ring", [P, CT], I32)
        work = sb("work", [P, max(CT * T * WIN, 4 * XB * D)])
        hot = work[:, 0:CT * T * WIN].rearrange("p (c k) -> p c k", k=T * WIN)
        xin = work[:, 0:2 * XB * D].rearrange("p (a j d) -> p a j d", a=2, d=D)
        xt = work[:, 2 * XB * D:4 * XB * D].rearrange("p (a j n) -> p a j n", a=2, n=P)
        hot_iota = sb("hot_iota", [P, T * WIN])
        stats = sb("stats", [NI, ST])
        neg_base = sb("neg_base", [NI, NG])
        top = sb("top", [NI, NG])
        back = sb("back", [NI, NG])
        limit = sb("limit", [NI, NG])
        esrc_raw = sb("esrc_raw", [ET, P], I32)
        edst_raw = sb("edst_raw", [ET, P], I32)
        etyp_raw = sb("etyp_raw", [ET, P], I32)
        esrc_f = sb("esrc_f", [ET, P])
        eidx_f = sb("eidx_f", [ET, P])
        ekey_f = sb("ekey_f", [ET, P])
        esrc_first = sb("esrc_first", [P, PRE], I32)
        esrc_t = sb("esrc_t", [P, ET], I32)
        eidx_t = sb("eidx_t", [P, ET], I32)
        ekey_t = sb("ekey_t", [P, ET])
        estats = sb("estats", [ET, EST])
        etop = sb("etop", [ET, 1])
        xg = sb("xg", [P, ET, D])
        xs = sb("xs", [P, 2, D])
        xst = sb("xst", [P, 2, P])
        emsg = sb("emsg", [P, 2, T * D])
        ehot = sb("ehot", [P, 2, T * WIN])
        row_f = sb("row_f", [1, STATS])
        row_i = sb("row_i", [1, STATS], I32)
        ctl_f = sb("ctl_f", [1, 10])
        ctl = sb("ctl", [1, 2], I32)
        tab = sb("tab", [P, 2, XB, T * D])
        msg = tab[:, :, :, :].rearrange("p a j c -> p (a j c)")[:, 0:CT * D].rearrange("p (c d) -> p c d", d=D)
        we_raw = sb("we_raw", [P, T, D])
        wn_raw = sb("wn_raw", [P, T, (T + 1) * D])
        we_t = sb("we_t", [P, T * D])
        wn_t = sb("wn_t", [P, T + 1, T * D])
        be_b = sb("be_b", [P, T * D])
        bn_row = sb("bn_row", [1, T * D])
        ones = sb("ones", [1, P])
        zero = sb("zero", [P, 1])
        ident = sb("ident", [P, P])
        nt_raw = sb("nt_raw", [NT, P], I32)
        nt_f = sb("nt_f", [NT, P])
        nt_t = sb("nt_t", [P, NT])
        mask = sb("mask", [P, T, NT])
        x_fin = [sb(f"x_fin{z}", [P, D]) for z in range(2)]
        stage = [sb(f"stage{z}", [P, T + 1, P]) for z in range(2)]
        h = [sb(f"h{z}", [P, D]) for z in range(2)]
        y = [sb(f"y{z}", [P, D]) for z in range(2)]
        bnst = [sb(f"bnst{z}", [P, 6]) for z in range(2)]
        mv = [sb(f"mv{z}", [P, 2]) for z in range(2)]
        sd = [sb(f"sd{z}", [P, 1]) for z in range(2)]
        rstd = [sb(f"rstd{z}", [P, 1]) for z in range(2)]
        eps = sb("eps", [P, 1])
        ps = ctx.enter_context(nc.psum_tensor("ps", [P, 8, 512], F32))

        got_esrc, got_early, got_edges = sem("got_esrc"), sem("got_early"), sem("got_edges")
        got_we, got_wn, got_be, got_bn, got_nt = (sem("got_we"), sem("got_wn"), sem("got_be"), sem("got_bn"),
                                                  sem("got_nt"))
        got_first = [sem(f"got_first{q}") for q in range(PRE)]
        got_x = [sem("got_x0"), sem("got_x1")]
        esrc_pad_set = sem("esrc_pad_set")
        pads_set, ident_set, consts_set, zero_set = (sem("pads_set"), sem("ident_set"), sem("consts_set"),
                                                     sem("zero_set"))
        hot_iota_set, acc_zeroed, limits_set = sem("hot_iota_set"), sem("acc_zeroed"), sem("limits_set")
        esrc_cast, early_set, nt_cast, masks_set = (sem("esrc_cast"), sem("early_set"), sem("nt_cast"),
                                                    sem("masks_set"))
        rows_set, bases_set, keys_set = sem("rows_set"), sem("bases_set"), sem("keys_set")
        keys_shifted, stats_set = sem("keys_shifted"), sem("stats_set")
        stats_out, stats_in, ctl_set = sem("stats_out"), sem("stats_in"), sem("ctl_set")
        setup_t, setup_copied = sem("setup_t"), sem("setup_copied")
        vec_step = sem("vec_step")
        x_turned, xt_copied, msg_made = sem("x_turned"), sem("xt_copied"), sem("msg_made")
        biased, tab_ready = sem("biased"), sem("tab_ready")
        tab_stored = [sem(f"tab_stored{h}") for h in range(4)]
        hot_ready, idx_ready = sem("hot_ready"), sem("idx_ready")
        gathered = [sem(f"gathered{g}") for g in range(NG)]
        group_summed, group_added = sem("group_summed"), sem("group_added")
        x_gathered_pre, x_gathered, e_staged, e_turned, e_copied, e_made = (
            sem("x_gathered_pre"), sem("x_gathered"), sem("e_staged"), sem("e_turned"), sem("e_copied"), sem("e_made"))
        e_biased, e_ready, e_hot, e_summed, e_added = (
            sem("e_biased"), sem("e_ready"), sem("e_hot"), sem("e_summed"), sem("e_added"))
        def two(name):
            return [sem(name + "0"), sem(name + "1")]

        fin_x, fin_xt, stage_xt, stage_acc, fin_lin = (two("fin_x"), two("fin_xt"), two("stage_xt"),
                                                       two("stage_acc"), two("fin_lin"))
        fin_step, fin_var, fin_sd, fin_y, stored = (two("fin_step"), two("fin_var"), two("fin_sd"),
                                                    two("fin_y"), two("stored"))
        FIN_STEPS = 6
        gen_shift, gen_ready, gen_summed, gen_added, gen_done = (
            sem("gen_shift"), sem("gen_ready"), sem("gen_summed"), sem("gen_added"), sem("gen_done"))
        gen_gathered = [sem(f"gen_gathered{g}") for g in range(NG)]
        gen_gathered_early = sem("gen_gathered_early")
        SHIFTS = 4
        GEN = NI * NG + ET
        MAX_PASSES = N // WIN + 3

        KP = 512 // NI
        UNITS = ([("esrc", 1, ET), ("we", T, P)] + [("wn", T, P)] * (T + 1)
                 + [("nt", 1, NT), ("ekey", 1, ET), ("eidx", 1, ET)]
                 + [("key", KP, NI), ("key", CT - KP, NI), ("idx", KP, NI), ("idx", CT - KP, NI)])
        UNITS_AFTER = [(2, 4), (4, 6), (6, 9), (9, len(UNITS))]

        block = ctx.enter_context(nc.Block())

        def hold(engine):
            engine.nop(nofuse=True)

        def at(j):
            return slice(j, j + 1) if isinstance(j, int) else bass.ds(j, 1)

        def load_x(engine, b, par):
            engine.dma_start(xin[:, par, :, :],
                             x[bass.ds(b * (XB * P), XB * P), :].rearrange("(j p) d -> p j d", p=P)
                             ).then_inc(got_x[par], 16)

        @block.sync
        def _(sp):
            def load_early(raw, dram, signal):
                first = MAIN
                sp.dma_start(raw[0:ET - 1, :], dram[first:first + (ET - 1) * P].rearrange("(p c) -> p c", c=P)
                             ).then_inc(signal, 16)
                sp.dma_start(raw[ET - 1:ET, 0:ELAST], dram[E - ELAST:E].rearrange("(p c) -> p c", p=1)
                             ).then_inc(signal, 16)

            for q in range(PRE):
                sp.dma_start(esrc_first[:, q:q + 1], src[MAIN + q * P:MAIN + (q + 1) * P].rearrange("(p c) -> p c", c=1)
                             ).then_inc(got_first[q], 16)
            sp.wait_ge(esrc_pad_set, 1)
            load_early(esrc_raw, src, got_esrc)
            load_x(sp, 0, 0)
            load_x(sp, 1, 1)
            sp.wait_ge(pads_set, 5)
            for raw, dram in ((edst_raw, dst), (etyp_raw, etype)):
                load_early(raw, dram, got_early)
            for raw, dram in ((dst_raw, dst), (src_raw, src), (typ_raw, etype)):
                sp.dma_start(raw[0:NI - 1, :], dram[0:(NI - 1) * ROW].rearrange("(p c) -> p c", c=ROW)
                             ).then_inc(got_edges, 16)
                sp.dma_start(raw[NI - 1:NI, 0:LAST_COL], dram[(NI - 1) * ROW:MAIN].rearrange("(p c) -> p c", p=1)
                             ).then_inc(got_edges, 16)
            for c in range(LAST_COL, ROW, P):
                sp.dma_start(dst_raw[NI - 1:NI, c:c + P], dst[MAIN - P:MAIN].rearrange("(p c) -> p c", p=1)
                             ).then_inc(got_edges, 16)

            def store_half(b, par, half, tiles=XH, rows=P):
                sp.wait_ge(tab_ready, 2 * b + half + 1)
                dest = table[bass.ds(b * (XB * P * T) + half * (XH * P * T), tiles * rows * T), :]
                sp.dma_start(dest.rearrange("(j p t) d -> p j (t d)", p=rows, t=T),
                             tab[0:rows, par, half * XH:half * XH + tiles, :]
                             ).then_inc(tab_stored[2 * par + half], 16)

            with sp.Fori(0, NB // 2) as k:
                for par in range(2):
                    for half in range(2):
                        store_half(2 * k + par, par, half)
            sp.wait_ge(stats_set, 2)
            sp.dma_start(stats_dram[0:NI * ST].rearrange("(p c) -> p c", c=ST), stats[:, :]
                         ).then_inc(stats_out, 16)
            sp.dma_start(stats_dram[NI * ST:STATS].rearrange("(p c) -> p c", c=EST), estats[:, :]
                         ).then_inc(stats_out, 16)
            sp.wait_ge(stats_out, 32)
            sp.dma_start(row_f[:, :], stats_dram.rearrange("(a c) -> a c", a=1)).then_inc(stats_in, 16)
            store_half(NB, 0, 0, tiles=1, rows=TAIL)

            def load_fin(j, z=0, rows=P):
                sp.dma_start(x_fin[z][0:rows, :], x[bass.ds(j * P, rows), :]).then_inc(fin_x[z], 16)

            def store_fin(j, nth, z=0, rows=P):
                sp.wait_ge(fin_y[z], nth + 1)
                sp.dma_start(out[bass.ds(j * P, rows), :], y[z][0:rows, :]).then_inc(stored[z], 16)

            sp.wait_ge(consts_set, 2)
            load_fin(0)
            load_fin(ORDER[0], 1, TAIL)
            with sp.Fori(0, NE - 1) as j:
                store_fin(j, j)
                load_fin(j + 1)
            for n in range(KE):
                store_fin(ORDER[n], n, 1, P if n else TAIL)
                load_fin(ORDER[n + 1], 1)
                store_fin(NE - 1 + n, NE - 1 + n)
                load_fin(NE + n)
            with sp.Fori(NE + KE - 1, NA - 1) as j:
                store_fin(j, j)
                load_fin(j + 1)
            store_fin(NA - 1, NA - 1)
            store_fin(ORDER[KE], KE, 1)
            sp.wait_ge(stored[0], NA * 16)
            sp.wait_ge(stored[1], NZ * 16)
            sp.wait_ge(ctl_set, 1)
            need = sp.value_load(ctl[0:1, 0:1], min_val=0, max_val=1)
            with sp.If(need > 0):
                load_fin(0)
                with sp.Fori(0, NT - 2) as j:
                    store_fin(j, j + NA)
                    load_fin(j + 1)
                store_fin(NT - 2, NT - 2 + NA)
                load_fin(NT - 1, 0, TAIL)
                store_fin(NT - 1, NT - 1 + NA, 0, TAIL)
                sp.wait_ge(stored[0], (NA + NT) * 16)

        @block.gpsimd
        def _(pool):
            pool.memset(esrc_raw[:, ELAST:P], 0).then_inc(esrc_pad_set, 1)
            pool.memset(edst_raw[:, ELAST:P], N - 1).then_inc(pads_set, 1)
            pool.memset(etyp_raw[:, ELAST:P], T).then_inc(pads_set, 1)
            pool.memset(nt_raw[:, TAIL:P], 0).then_inc(pads_set, 1)
            pool.memset(src_raw[:, LAST_COL:ROW], 0).then_inc(pads_set, 1)
            pool.memset(typ_raw[:, LAST_COL:ROW], T).then_inc(pads_set, 1)
            pool.memset(ident[:, :], 0.0).then_inc(ident_set, 1)
            pool.memset(zero[:, :], 0.0).then_inc(zero_set, 1)
            pool.wait_ge(ident_set, 1)
            pool.affine_select(out=ident[:, :], in_=ident[:, :], compare_op=ALU.not_equal, fill=1.0, base=0,
                               pattern=[[-1, P]], channel_multiplier=1).then_inc(ident_set, 1)
            pool.iota(limit[:, 0:FIN + 1], pattern=[[0, FIN + 1]], base=-P, channel_multiplier=P,
                      allow_small_or_imprecise_dtypes=True)
            pool.iota(limit[:, FIN + 1:NG], pattern=[[0, NG - FIN - 1]], base=0, channel_multiplier=P,
                      allow_small_or_imprecise_dtypes=True).then_inc(limits_set, 1)
            pool.iota(hot_iota[:, :], pattern=[[TYPE_STEP, T], [1, WIN]], base=0, channel_multiplier=0,
                      allow_small_or_imprecise_dtypes=True).then_inc(hot_iota_set, 1)
            pool.memset(ones[:, :], 1.0)
            pool.memset(eps[:, :], EPS).then_inc(consts_set, 1)

            for q in range(ET):
                if q < PRE:
                    pool.wait_ge(got_first[q], 16)
                if q == PRE:
                    pool.wait_ge(setup_copied, 1)
                rows = (esrc_first if q < PRE else esrc_t)[:, q:q + 1]
                pool.indirect_dma_start(xg[:, q, :], None, x, bass.IndirectOffsetOnAxis(ap=rows, axis=0)
                                        ).then_inc(x_gathered_pre if q < PRE else x_gathered, 16)

            def gather(slot, signal):
                pool.indirect_dma_start(msg[:, slot, :], None, table,
                                        bass.IndirectOffsetOnAxis(ap=idx_ring[:, slot:slot + 1], axis=0)
                                        ).then_inc(signal, 16)

            pool.wait_ge(tab_stored[0], (NB // 2 + 1) * 16)
            for half in range(1, 4):
                pool.wait_ge(tab_stored[half], NB // 2 * 16)

            def iteration(j, sizes):
                for g in range(NG):
                    pool.wait_ge(idx_ready, NG * j + g + 1)
                    hold(pool)
                    for c in range(sizes[g]):
                        gather(FIRST[g] + c, gathered[g])

            with pool.Fori(0, NI - 1) as j:
                iteration(j, SIZES)
            iteration(NI - 1, LAST_SIZES)

            pool.wait_ge(ctl_set, 1)
            need = pool.value_load(ctl[0:1, 0:1], min_val=0, max_val=1)
            with pool.If(need > 0):
                passes = pool.value_load(ctl[0:1, 1:2], min_val=1, max_val=MAX_PASSES)
                with pool.Fori(0, passes) as k:
                    with pool.Fori(0, NI) as j:
                        for g in range(NG):
                            pool.wait_ge(gen_ready, 2 * (k * GEN + j * NG + g + 1))
                            hold(pool)
                            for c in range(SIZES[g]):
                                gather(FIRST[g] + c, gen_gathered[g])
                    with pool.Fori(0, ET) as q:
                        pool.wait_ge(gen_ready, 2 * (k * GEN + NI * NG + q + 1))
                        hold(pool)
                        gather(0, gen_gathered_early)

        @block.scalar
        def _(act):
            act.dma_start(we_raw[:, :, :], w_e.rearrange("t o i -> o t i")).then_inc(got_we, 16)
            act.dma_start(be_b[:, :], b_e.rearrange("(a t) o -> a (t o)", a=1).broadcast_to((P, T * D))
                          ).then_inc(got_be, 16)

            def setup_copy(first, last):
                for u in range(first, last):
                    name, pieces, width = UNITS[u]
                    bank = ps[:, SETUP_BANKS[u % 2], 0:pieces * width]
                    nth = sum(UNITS[i][0] == name for i in range(u))
                    if name == "wn":
                        dest = wn_t[:, nth, :]
                    elif name in ("key", "idx"):
                        whole = key_t if name == "key" else idx_t
                        dest = whole[:, :, :].rearrange("p j c -> p c j")[:, KP * nth:KP * nth + pieces, :]
                        bank = bank.rearrange("p (c j) -> p c j", j=NI)
                    else:
                        dest = {"esrc": esrc_t, "we": we_t, "nt": nt_t, "ekey": ekey_t, "eidx": eidx_t}[name][:, :]
                    act.wait_ge(setup_t, u + 1)
                    act.activation(dest, bank, ACT.Copy).then_inc(setup_copied, 1)

            def copy_xt(b, par, first=False, load="batch"):
                act.wait_ge(x_turned, b + 1)
                if load == "batch":
                    if not isinstance(b, int):
                        hold(act)
                    load_x(act, b + 2, par)
                elif load == "tail":
                    act.dma_start(xin[0:TAIL, par, 0, :], x[(NT - 1) * P:N, :]).then_inc(got_x[par], 16)
                if not first:
                    act.wait_ge(msg_made, XB * (b - 1))
                act.activation(xt[:, par, :, :], ps[:, XT_PS[par], :].rearrange("p (j n) -> p j n", n=P),
                               ACT.Copy).then_inc(xt_copied, 1)

            def relu_half(b, par, half, tiles=XH):
                act.wait_ge(biased, XB * b + half * XH + tiles)
                part = tab[:, par, half * XH:half * XH + tiles, :]
                act.activation(part, part, ACT.Relu).then_inc(tab_ready, 1)

            def relu_batch(b, par):
                relu_half(b, par, 0)
                relu_half(b, par, 1)

            def zero_acc(part, n):
                act.activation(part, zero[:, 0:1].broadcast_to((P, n)), ACT.Copy).then_inc(acc_zeroed, 1)

            act.wait_ge(zero_set, 1)
            act.activation(x_fin[1][:, :], zero[:, 0:1].broadcast_to((P, D)), ACT.Copy).then_inc(consts_set, 1)
            setup_copy(0, 1)
            act.dma_start(wn_raw[:, :, :], w_n.rearrange("t o i -> o t i")).then_inc(got_wn, 16)
            act.dma_start(bn_row[:, :], b_n.rearrange("(a t) o -> a (t o)", a=1)).then_inc(got_bn, 16)
            act.wait_ge(pads_set, 5)
            act.dma_start(nt_raw[0:NT - 1, :], ntype[0:(NT - 1) * P].rearrange("(p c) -> p c", c=P)
                          ).then_inc(got_nt, 16)
            act.dma_start(nt_raw[NT - 1:NT, 0:TAIL], ntype[(NT - 1) * P:N].rearrange("(p c) -> p c", p=1)
                          ).then_inc(got_nt, 16)
            zero_acc(acc[:, 1, 0:ZC], ZC)
            setup_copy(1, 2)
            copy_xt(0, 0, first=True)
            copy_xt(1, 1, first=True)
            for b in range(PEELED):
                if b == 3:
                    setup_copy(*UNITS_AFTER[b])
                relu_batch(b, b % 2)
                if b + 2 <= PEELED:
                    copy_xt(b + 2, b % 2)
                if b < 3:
                    setup_copy(*UNITS_AFTER[b])
                if b == 2:
                    act.wait_ge(bases_set, NG + 1)
                    act.wait_ge(keys_set, 1)
                    for g in range(NG):
                        span = slice(FIRST[g] * P, (FIRST[g] + SIZES[g]) * P)
                        act.activation(key_f[:, span], key_f[:, span], ACT.Identity, bias=neg_base[:, g:g + 1]
                                       ).then_inc(keys_shifted, 1)

            def batch(b, par, load="batch"):
                copy_xt(b + 1, 1 - par, load=load)
                relu_batch(b, par)
                zero_acc(acc[:, 2, bass.ds((b - PEELED) * ZC, ZC)], ZC)

            with act.Fori(PEELED // 2, NB // 2 - 2) as k:
                for par in range(2):
                    batch(2 * k + par, par)
            for b in range(NB - 4, NB):
                batch(b, b % 2, load={NB - 4: "batch", NB - 3: "tail"}.get(b))
            relu_half(NB, 0, 0, 1)

            def early_stage(q, slot, first=False):
                if not first:
                    act.wait_ge(e_turned, q - 1)
                    hold(act)
                act.activation(xs[:, slot, :], xg[:, at(q), :].rearrange("p a d -> p (a d)"), ACT.Copy
                               ).then_inc(e_staged, 1)

            def early_copy(q, slot, first=False):
                if not first:
                    act.wait_ge(e_made, q - 1)
                act.wait_ge(e_turned, q + 1)
                act.activation(xst[:, slot, :], ps[:, E_XT_PS, 0:P], ACT.Copy
                               ).then_inc(e_copied, 1)

            def early_relu(q, slot):
                act.wait_ge(e_biased, q + 1)
                act.activation(emsg[:, slot, :], emsg[:, slot, :], ACT.Relu).then_inc(e_ready, 1)

            def finish_x(nth, z=0, first=False):
                act.wait_ge(fin_xt[z], nth + 1)
                if not first:
                    act.wait_ge(fin_lin[z], nth)
                act.activation(stage[z][:, 0, :], ps[:, FIN_XT_PS[z], 0:P], ACT.Relu).then_inc(stage_xt[z], 1)

            def finish_acc(tile, z=0, added=None):
                if added is not None:
                    act.wait_ge(group_added, added)
                    hold(act)
                act.activation(stage[z][:, 1:T + 1, :], acc[:, :, bass.ds(tile * P, P)], ACT.Copy
                               ).then_inc(stage_acc[z], 1)

            def finish_sd(nth, z=0):
                act.wait_ge(fin_var[z], nth + 1)
                act.activation(sd[z][:, :], mv[z][:, 1:2], ACT.Sqrt, bias=eps[:, :]).then_inc(fin_sd[z], 1)

            def iteration(j, early=False, fin=True, extra=None, last=False):
                q = PRE + 2 * j
                if last:
                    finish_x(KE, 1)
                if extra is not None:
                    finish_x(extra, 1, first=extra == 0)
                    finish_acc(ORDER[extra], 1, NG * j + 1)
                if early:
                    early_stage(q, SLOTS[0])
                    early_copy(q, SLOTS[0])
                    early_relu(q, SLOTS[0])
                    early_stage(q + 1, SLOTS[1])
                    early_copy(q + 1, SLOTS[1])
                if fin:
                    finish_x(j - 1, first=isinstance(j, int) and j == 1)
                    finish_acc(j - 1, added=NG * j + FIN + 1)
                if early:
                    early_relu(q + 1, SLOTS[1])
                if last:
                    finish_acc(ORDER[KE], 1, NG * NI)
                if extra is not None:
                    finish_sd(extra, 1)
                if fin:
                    finish_sd(j - 1)
                if last:
                    finish_sd(KE, 1)

            act.wait_ge(consts_set, 2)
            act.wait_ge(x_gathered_pre, 16 * PRE)
            for q in range(PRE):
                early_stage(q, q % 2, first=q < 2)
                early_copy(q, q % 2, first=q < 2)
                early_relu(q, q % 2)
            act.wait_ge(x_gathered, 16 * (ET - PRE))
            iteration(0, True, False)
            iteration(1, True)
            with act.Fori(2, NE) as j:
                iteration(j, True)
            for n in range(KE):
                iteration(NE + n, extra=n)
            with act.Fori(NE + KE, NI - 1) as j:
                iteration(j)
            iteration(NI - 1, last=True)

            act.wait_ge(ctl_set, 1)
            need = act.value_load(ctl[0:1, 0:1], min_val=0, max_val=1)
            with act.If(need > 0):
                act.wait_ge(gen_done, 1)
                with act.Fori(0, NT) as j:
                    finish_x(j + NA)
                    finish_acc(j)
                    finish_sd(j + NA)

        @block.vector
        def _(dve):
            steps = [0]

            def link(ins):
                steps[0] += 1
                ins.then_inc(vec_step, 1)
                dve.wait_ge(vec_step, steps[0])

            dve.memset(acc[:, 1, HALF:NPAD], 0.0).then_inc(acc_zeroed, 1)
            dve.wait_ge(got_esrc, 32)
            dve.tensor_copy(esrc_f[:, :], esrc_raw[:, :]).then_inc(esrc_cast, 1)
            dve.memset(acc[:, 1, ZC:HALF], 0.0).then_inc(acc_zeroed, 1)

            def early_prep():
                dve.wait_ge(got_early, 64)
                dve.wait_ge(esrc_cast, 1)
                dve.tensor_reduce(estats[:, 0:1], edst_raw[:, :], AX.X, ALU.min)
                dve.tensor_reduce(etop[:, :], edst_raw[:, :], AX.X, ALU.max)
                dve.scalar_tensor_tensor(ekey_f[:, :], etyp_raw[:, :], float(TYPE_STEP), edst_raw[:, :],
                                         ALU.mult, ALU.add)
                link(dve.scalar_tensor_tensor(eidx_f[:, :], esrc_f[:, :], float(T), etyp_raw[:, :],
                                              ALU.mult, ALU.add))
                dve.tensor_scalar(eidx_f[:, :], eidx_f[:, :], float(N * T - 1), None, ALU.min)
                dve.tensor_tensor(estats[:, 1:2], etop[:, :], estats[:, 0:1], ALU.subtract)
                dve.tensor_scalar(estats[:, 2:3], estats[:, 0:1], -1.0, float(EARLY_BACK), ALU.mult, ALU.add
                                  ).then_inc(stats_set, 1)
                dve.tensor_scalar(ekey_f[:, :], ekey_f[:, :], estats[:, 0:1], None, ALU.subtract
                                  ).then_inc(early_set, 1)

            def spans(signal, out, op):
                for g in range(NG):
                    span = slice(FIRST[g] * P, (FIRST[g] + SIZES[g]) * P)
                    dve.tensor_reduce(out[:, g:g + 1], dst_raw[:, span], AX.X, op).then_inc(signal, 1)

            def bases():
                dve.wait_ge(got_edges, 16 * EDGE_LOADS)
                spans(bases_set, stats, ALU.min)
                dve.wait_ge(bases_set, NG)
                dve.tensor_scalar(neg_base[:, :], stats[:, 0:NG], -1.0, None, ALU.mult).then_inc(bases_set, 1)

            def table_rows():
                dve.scalar_tensor_tensor(idx_f, src_raw[:, :], float(T), typ_raw[:, :], ALU.mult, ALU.add
                                         ).then_inc(rows_set, 1)

            def keys():
                dve.wait_ge(rows_set, 1)
                dve.scalar_tensor_tensor(key_f, typ_raw[:, :], float(TYPE_STEP), dst_raw[:, :], ALU.mult, ALU.add
                                         ).then_inc(keys_set, 1)

            def reach():
                spans(vec_step, top, ALU.max)
                steps[0] += NG
                dve.wait_ge(vec_step, steps[0])
                dve.wait_ge(limits_set, 1)
                dve.tensor_reduce(stats[:, NG + 2:NG + 3], top[:, :], AX.X, ALU.max)
                dve.tensor_tensor(back[:, :], limit[:, :], stats[:, 0:NG], ALU.subtract)
                link(dve.tensor_tensor(neg_base[:, :], top[:, :], stats[:, 0:NG], ALU.subtract))
                dve.tensor_scalar(stats[:, NG + 2:NG + 3], stats[:, NG + 2:NG + 3], float(AHEAD), None, ALU.subtract)
                dve.tensor_reduce(stats[:, NG:NG + 1], neg_base[:, :], AX.X, ALU.max)
                dve.tensor_reduce(stats[:, NG + 1:NG + 2], back[:, :], AX.X, ALU.max).then_inc(stats_set, 1)

            def bias_batch(b, par, tiles=XB, rest=None):
                for i in range(tiles):
                    if rest is not None and i % XH == 0:
                        dve.wait_ge(tab_stored[2 * par + i // XH], rest)
                    dve.wait_ge(msg_made, XB * b + i + 1)
                    dve.tensor_tensor(tab[:, par, i, :], ps[:, MSG_PS + i, 0:T * D], be_b[:, :], ALU.add
                                      ).then_inc(biased, 1)

            early_prep()
            dve.wait_ge(got_be, 16)
            bias_batch(0, 0)
            dve.wait_ge(got_nt, 32)
            dve.tensor_copy(nt_f[:, :], nt_raw[:, :]).then_inc(nt_cast, 1)
            bases()
            bias_batch(1, 1)
            table_rows()
            bias_batch(2, 0, rest=16)
            keys()
            bias_batch(3, 1, rest=16)
            dve.wait_ge(keys_shifted, NG)
            reach()
            def load_rows(j, g, n, signal):
                dve.tensor_copy(idx_ring[:, FIRST[g]:FIRST[g] + n], idx_t[:, j, FIRST[g]:FIRST[g] + n]
                                ).then_inc(signal, 1)

            dve.wait_ge(setup_copied, len(UNITS))
            for g in range(NG):
                load_rows(0, g, SIZES[g], idx_ready)
            with dve.Fori(PEELED // 2, NB // 2) as k:
                for par in range(2):
                    bias_batch(2 * k + par, par, rest=16 * k)
                    dve.wait_ge(zero_set, 1)
                    dve.tensor_copy(acc[:, 0, bass.ds((2 * k + par - PEELED) * ZC, ZC)],
                                    zero[:, 0:1].broadcast_to((P, ZC))).then_inc(acc_zeroed, 1)
            bias_batch(NB, 0, 1, rest=16 * (NB // 2))

            for t in range(T):
                ins = dve.tensor_scalar(mask[:, t, :], nt_t[:, :], float(t), None, ALU.is_equal)
            ins.then_inc(masks_set, 1)

            def one_hot(j, g, n, signal):
                keys = key_t[:, j, FIRST[g]:FIRST[g] + n].rearrange("p (c o) -> p c o", o=1)
                dve.tensor_tensor(hot[:, FIRST[g]:FIRST[g] + n, :], keys.broadcast_to((P, n, T * WIN)),
                                  hot_iota[:, :].rearrange("p (o c) -> p o c", o=1).broadcast_to((P, n, T * WIN)),
                                  ALU.is_equal).then_inc(signal, 1)

            def add_sums(bank, base, signal):
                cols = acc[:, :, bass.ds(base, WIN)]
                dve.tensor_tensor(cols, bank.rearrange("p (t c) -> p t c", t=T), cols, ALU.add).then_inc(signal, 1)

            def group_bank(g):
                return ps[:, AGG[g], 0:T * WIN]

            early_bank = ps[:, E_SUM_PS, 0:T * WIN]

            dve.wait_ge(hot_iota_set, 1)
            for g in range(NG):
                one_hot(0, g, SIZES[g], hot_ready)

            dve.wait_ge(stats_in, 16)
            rows = row_f[:, 0:NI * ST].rearrange("a (j s) -> a s j", s=ST)
            erows = row_f[:, NI * ST:STATS].rearrange("a (j s) -> a s j", s=EST)
            dve.tensor_copy(row_i[:, :], row_f[:, :])
            for s in range(3):
                dve.tensor_reduce(ctl_f[:, s:s + 1], rows[:, NG + s, :], AX.X, ALU.max)
            dve.tensor_reduce(ctl_f[:, 3:4], erows[:, 1, :], AX.X, ALU.max)
            link(dve.tensor_reduce(ctl_f[:, 4:5], erows[:, 2, :], AX.X, ALU.max))
            dve.tensor_tensor(ctl_f[:, 5:6], ctl_f[:, 0:1], ctl_f[:, 3:4], ALU.max)
            dve.tensor_tensor(ctl_f[:, 6:7], ctl_f[:, 1:2], ctl_f[:, 4:5], ALU.max)
            link(dve.tensor_scalar(ctl_f[:, 7:8], ctl_f[:, 2:3], 0.5, None, ALU.is_gt))
            dve.tensor_scalar(ctl_f[:, 8:9], ctl_f[:, 5:6], float(WIN) - 0.5, None, ALU.is_gt)
            dve.tensor_scalar(ctl_f[:, 9:10], ctl_f[:, 6:7], 0.5, None, ALU.is_gt)
            link(dve.tensor_scalar(ctl_f[:, 5:6], ctl_f[:, 5:6], 1.0 / WIN, 1.0, ALU.mult, ALU.add))
            link(dve.tensor_tensor(ctl_f[:, 8:9], ctl_f[:, 8:9], ctl_f[:, 9:10], ALU.max))
            dve.tensor_tensor(ctl[:, 0:1], ctl_f[:, 7:8], ctl_f[:, 8:9], ALU.max)
            link(dve.tensor_copy(ctl[:, 1:2], ctl_f[:, 5:6]))
            dve.nop().then_inc(ctl_set, 1)
            dve.wait_ge(acc_zeroed, 1 + 1 + 1 + 8 + 8)

            def early_hot(q, slot, first=False):
                if not first:
                    dve.wait_ge(e_summed, q - 1)
                dve.tensor_scalar(ehot[:, slot, :], hot_iota[:, :], ekey_t[:, at(q)], None, ALU.is_equal
                                  ).then_inc(e_hot, 1)

            def early_bias(q, slot):
                dve.wait_ge(e_made, q + 1)
                dve.tensor_tensor(emsg[:, slot, :], ps[:, E_MSG_PS, 0:T * D], be_b[:, :], ALU.add
                                  ).then_inc(e_biased, 1)

            def early_base(q):
                return dve.value_load(row_i[0:1, at(NI * ST + EST * q)], min_val=0, max_val=N - 1)

            def early_add(q, groups=None):
                dve.wait_ge(e_summed, q + 1)
                base = early_base(q)
                if groups is not None:
                    dve.wait_ge(group_added, groups)
                elif q:
                    dve.wait_ge(e_added, q)
                add_sums(early_bank, base, e_added)

            def finish(tile, nth, z=0, first=False):
                done = [0]

                def fin_link(ins):
                    done[0] += 1
                    ins.then_inc(fin_step[z], 1)
                    dve.wait_ge(fin_step[z], nth * FIN_STEPS + done[0])

                dve.wait_ge(fin_x[z], 16 * (nth + 1))
                fin_link(dve.tensor_tensor(h[z][:, :], x_fin[z][:, :], x_fin[z][:, :], ALU.add))
                dve.wait_ge(fin_lin[z], nth + 1)
                for t in range(T):
                    fin_link(dve.scalar_tensor_tensor(h[z][:, :], ps[:, LIN_PS[z], t * D:(t + 1) * D],
                                                      mask[:, t, at(tile)], h[z][:, :], ALU.mult, ALU.add))
                fin_link(dve.bn_stats(bnst[z][:, :], h[z][:, :]))
                hold(dve)
                dve.bn_aggr(mv[z][:, :], bnst[z][:, :]).then_inc(fin_var[z], 1)
                dve.wait_ge(fin_sd[z], nth + 1)
                fin_link(dve.reciprocal(rstd[z][:, :], sd[z][:, :]))
                dve.wait_ge(fin_var[z], nth + 1)
                if not first:
                    dve.wait_ge(stored[z], 16 * nth)
                dve.tensor_scalar(y[z][:, :], h[z][:, :], mv[z][:, 0:1], rstd[z][:, :], ALU.subtract, ALU.mult
                                  ).then_inc(fin_y[z], 1)
                assert done[0] == FIN_STEPS

            def iteration(j, early=False, fin=True, extra=None, first_plain=False, next_sizes=SIZES):
                q = PRE + 2 * j
                if early:
                    early_hot(q, SLOTS[0])
                    early_hot(q + 1, SLOTS[1])
                for g in range(NG):
                    dve.wait_ge(group_summed, NG * j + g + 1)
                    if next_sizes:
                        load_rows(j + 1, g, next_sizes[g], idx_ready)
                        one_hot(j + 1, g, next_sizes[g], hot_ready)
                    base = dve.value_load(row_i[0:1, at(j * ST + g)], min_val=0, max_val=N - 1)
                    if g in (FIN + 1, 0) and early:
                        dve.wait_ge(e_added, q + 1 if g else q)
                    elif g == 0 and first_plain:
                        dve.wait_ge(e_added, ET)
                        dve.wait_ge(group_added, NG * j + g)
                    else:
                        dve.wait_ge(group_added, NG * j + g)
                    if g == FIN + 1 and fin:
                        dve.wait_ge(stage_acc[0], j)
                    if g == 1 and extra is not None:
                        dve.wait_ge(stage_acc[1], extra + 1)
                    add_sums(group_bank(g), base, group_added)
                    if early and g == 1:
                        early_bias(q, SLOTS[0])
                    if early and g == FIN:
                        early_add(q, NG * j + g + 1)
                    if early and g == FIN + 1:
                        early_bias(q + 1, SLOTS[1])
                    if extra is not None and g == FIN:
                        finish(ORDER[extra], extra, 1, first=extra == 0)
                if early:
                    early_add(q + 1, NG * (j + 1))
                if fin:
                    finish(j - 1, j - 1, first=isinstance(j, int) and j == 1)

            for q in range(PRE):
                early_hot(q, q % 2, first=q < 2)
                early_bias(q, q % 2)
                early_add(q)
            iteration(0, True, False)
            iteration(1, True)
            with dve.Fori(2, NE) as j:
                iteration(j, True)
            for n in range(KE):
                iteration(NE + n, extra=n, first_plain=n == 0)
            with dve.Fori(NE + KE, NI - 2) as j:
                iteration(j)
            iteration(NI - 2, next_sizes=LAST_SIZES)
            iteration(NI - 1, next_sizes=None)
            finish(ORDER[KE], KE, 1)

            need = dve.value_load(ctl[0:1, 0:1], min_val=0, max_val=1)
            with dve.If(need > 0):
                passes = dve.value_load(ctl[0:1, 1:2], min_val=1, max_val=MAX_PASSES)
                dve.wait_ge(group_added, NG * NI)
                with dve.Fori(0, passes) as k:
                    dve.tensor_scalar(key_t[:, :, :], key_t[:, :, :], float(-WIN), None, ALU.add
                                      ).then_inc(gen_shift, 1)
                    dve.tensor_scalar(ekey_t[:, :], ekey_t[:, :], float(-WIN), None, ALU.add
                                      ).then_inc(gen_shift, 1)
                    dve.tensor_scalar(row_f[:, :], row_f[:, :], float(WIN), float(N), ALU.add, ALU.min
                                      ).then_inc(gen_shift, 1)
                    dve.wait_ge(gen_shift, k * SHIFTS + 3)
                    dve.tensor_copy(row_i[:, :], row_f[:, :]).then_inc(gen_shift, 1)
                    dve.wait_ge(gen_shift, k * SHIFTS + 4)
                    hold(dve)
                    with dve.Fori(0, NI) as j:
                        for g in range(NG):
                            nth = k * GEN + j * NG + g
                            load_rows(j, g, SIZES[g], gen_ready)
                            one_hot(j, g, SIZES[g], gen_ready)
                            dve.wait_ge(gen_summed, nth + 1)
                            base = dve.value_load(row_i[0:1, at(j * ST + g)], min_val=0, max_val=N)
                            add_sums(group_bank(g), base, gen_added)
                            dve.wait_ge(gen_added, nth + 1)
                            hold(dve)
                    with dve.Fori(0, ET) as q:
                        nth = k * GEN + NI * NG + q
                        dve.tensor_copy(idx_ring[:, 0:1], eidx_t[:, at(q)]).then_inc(gen_ready, 1)
                        dve.tensor_scalar(hot[:, 0, :], hot_iota[:, :], ekey_t[:, at(q)], None, ALU.is_equal
                                          ).then_inc(gen_ready, 1)
                        dve.wait_ge(gen_summed, nth + 1)
                        base = dve.value_load(row_i[0:1, at(NI * ST + EST * q)], min_val=0, max_val=N)
                        add_sums(group_bank(0), base, gen_added)
                        dve.wait_ge(gen_added, nth + 1)
                        hold(dve)
                dve.memset(ctl_f[:, 9:10], 0.0).then_inc(gen_done, 1)
                with dve.Fori(0, NT) as j:
                    finish(j, j + NA)

        @block.tensor
        def _(pe):
            def setup_unit(first, last):
                for u in range(first, last):
                    name, pieces, width = UNITS[u]
                    nth = sum(UNITS[i][0] == name for i in range(u))
                    if u >= len(SETUP_BANKS):
                        pe.wait_ge(setup_copied, u - len(SETUP_BANKS) + 1)
                    for i in range(pieces):
                        if name == "we":
                            piece = we_raw[:, i, :]
                        elif name == "wn":
                            piece = wn_raw[:, i, nth * D:(nth + 1) * D]
                        elif name in ("key", "idx"):
                            c = KP * nth + i
                            piece = (key_f if name == "key" else idx_f)[:, c * P:(c + 1) * P]
                        else:
                            piece = {"esrc": esrc_f, "nt": nt_f, "ekey": ekey_f, "eidx": eidx_f}[name][:, :]
                        ins = pe.transpose(ps[:, SETUP_BANKS[u % 2], i * width:(i + 1) * width], piece,
                                           ident[0:piece.shape[0], 0:piece.shape[0]])
                    ins.then_inc(setup_t, 1)

            def turn_batch(b, par, loads, first=False):
                pe.wait_ge(got_x[par], 16 * loads)
                if not first:
                    pe.wait_ge(xt_copied, b - 1)
                for i in range(XB):
                    ins = pe.transpose(ps[:, XT_PS[par], i * P:(i + 1) * P], xin[:, par, i, :], ident[:, :])
                ins.then_inc(x_turned, 1)

            def make_batch(b, par, tiles=XB, first=False):
                pe.wait_ge(xt_copied, b + 1)
                for i in range(tiles):
                    if not first:
                        pe.wait_ge(biased, XB * (b - 1) + i + 1)
                    pe.matmul(ps[:, MSG_PS + i, 0:T * D], xt[:, par, i, :], we_t[:, :], start=True, stop=True
                              ).then_inc(msg_made, 1)

            pe.wait_ge(ident_set, 2)
            pe.wait_ge(esrc_cast, 1)
            setup_unit(0, 1)
            pe.wait_ge(got_we, 16)
            setup_unit(1, 2)
            turn_batch(0, 0, 1, first=True)
            turn_batch(1, 1, 1, first=True)
            pe.wait_ge(setup_copied, 2)
            for b in range(PEELED):
                make_batch(b, b % 2, first=b == 0)
                if b + 2 <= PEELED:
                    turn_batch(b + 2, b % 2, b // 2 + 2)
                if b == 0:
                    pe.wait_ge(got_wn, 16)
                if b == 2:
                    pe.wait_ge(nt_cast, 1)
                    pe.wait_ge(early_set, 1)
                if b == 3:
                    pe.wait_ge(keys_shifted, NG)
                setup_unit(*UNITS_AFTER[b])
            with pe.Fori(PEELED // 2, NB // 2) as k:
                for par in range(2):
                    turn_batch(2 * k + par + 1, 1 - par, k + 1 + par)
                    make_batch(2 * k + par, par)
            make_batch(NB, 0, 1)

            def early_turn(q, slot, first=False):
                pe.wait_ge(e_staged, q + 1)
                if not first:
                    pe.wait_ge(e_copied, q)
                pe.transpose(ps[:, E_XT_PS, 0:P], xs[:, slot, :], ident[:, :]
                             ).then_inc(e_turned, 1)

            def early_make(q, slot, first=False):
                pe.wait_ge(e_copied, q + 1)
                if not first:
                    pe.wait_ge(e_biased, q)
                pe.matmul(ps[:, E_MSG_PS, 0:T * D], xst[:, slot, :], we_t[:, :], start=True, stop=True
                          ).then_inc(e_made, 1)

            def early_sum(q, slot, first=False):
                pe.wait_ge(e_ready, q + 1)
                pe.wait_ge(e_hot, q + 1)
                if not first:
                    pe.wait_ge(e_added, q)
                for t in range(T):
                    ins = pe.matmul(ps[:, E_SUM_PS, t * WIN:(t + 1) * WIN],
                                    emsg[:, slot, t * D:(t + 1) * D], ehot[:, slot, t * WIN:(t + 1) * WIN],
                                    start=True, stop=True)
                ins.then_inc(e_summed, 1)

            def sum_group(g, n, signal):
                for c in range(FIRST[g], FIRST[g] + n):
                    ins = pe.matmul(ps[:, AGG[g], 0:T * WIN], msg[:, c, :], hot[:, c, :],
                                    start=(c == FIRST[g]), stop=(c == FIRST[g] + n - 1))
                ins.then_inc(signal, 1)

            def finish_turn(nth, z=0, first=False):
                pe.wait_ge(fin_x[z], 16 * (nth + 1))
                if not first:
                    pe.wait_ge(stage_xt[z], nth)
                pe.transpose(ps[:, FIN_XT_PS[z], 0:P], x_fin[z][:, :], ident[:, :]).then_inc(fin_xt[z], 1)

            def linear_open(nth, z=0, first=False):
                lin = ps[:, LIN_PS[z], 0:T * D]
                pe.wait_ge(stage_xt[z], nth + 1)
                if not first:
                    pe.wait_ge(fin_y[z], nth)
                pe.matmul(lin, ones[:, :], bn_row[:, :], start=True, stop=False)
                pe.matmul(lin, stage[z][:, 0, :], wn_t[:, 0, :], start=False, stop=False)

            def linear_types(nth, z):
                lin = ps[:, LIN_PS[z], 0:T * D]
                pe.wait_ge(stage_acc[z], nth + 1)
                for i in range(1, T + 1):
                    ins = pe.matmul(lin, stage[z][:, i, :], wn_t[:, i, :], start=False, stop=(i == T))
                ins.then_inc(fin_lin[z], 1)

            def finish_linear(nth, z=0, first=False):
                linear_open(nth, z, first)
                linear_types(nth, z)

            def iteration(j, early=False, fin=True, extra=None, last=False):
                sizes = LAST_SIZES if last else SIZES
                q = PRE + 2 * j
                start = isinstance(j, int) and j == 1
                for g in range(NG):
                    if g > 2 or not (isinstance(j, int) and j == 0):
                        pe.wait_ge(group_added, NG * (j if g > 2 else j - 1) + BEFORE[g] + 1)
                    pe.wait_ge(hot_ready, NG * j + g + 1)
                    pe.wait_ge(gathered[g], SIZES[g] * 16 * j + sizes[g] * 16)
                    sum_group(g, sizes[g], group_summed)
                    if last:
                        if g == 0:
                            finish_turn(KE, 1)
                            linear_open(KE, 1)
                        if g == 1:
                            finish_turn(NA - 1)
                        if g == FIN:
                            linear_open(NA - 1)
                        continue
                    if g == 0:
                        if early:
                            early_turn(q, SLOTS[0])
                        if extra is not None:
                            finish_turn(extra, 1, extra == 0)
                    if g == 1:
                        if early:
                            early_make(q, SLOTS[0])
                        if extra is not None:
                            finish_linear(extra, 1, extra == 0)
                    if g == FIN:
                        if early:
                            early_sum(q, SLOTS[0])
                            early_turn(q + 1, SLOTS[1])
                        if fin:
                            finish_turn(j - 1, first=start)
                    if g == FIN + 1:
                        if early:
                            early_make(q + 1, SLOTS[1])
                        if fin:
                            finish_linear(j - 1, first=start)
                if early:
                    early_sum(q + 1, SLOTS[1])

            pe.wait_ge(consts_set, 2)
            pe.wait_ge(got_bn, 16)
            pe.wait_ge(masks_set, 1)
            pe.wait_ge(biased, XB * NB + 1)
            for q in range(PRE):
                early_turn(q, q % 2, first=q == 0)
                early_make(q, q % 2, first=q == 0)
                early_sum(q, q % 2, first=q == 0)
            iteration(0, True, False)
            iteration(1, True)
            with pe.Fori(2, NE) as j:
                iteration(j, True)
            for n in range(KE):
                iteration(NE + n, extra=n)
            with pe.Fori(NE + KE, NI - 1) as j:
                iteration(j)
            iteration(NI - 1, last=True)
            linear_types(NA - 1, 0)
            linear_types(KE, 1)

            pe.wait_ge(ctl_set, 1)
            need = pe.value_load(ctl[0:1, 0:1], min_val=0, max_val=1)
            with pe.If(need > 0):
                passes = pe.value_load(ctl[0:1, 1:2], min_val=1, max_val=MAX_PASSES)
                with pe.Fori(0, passes) as k:
                    with pe.Fori(0, NI) as j:
                        for g in range(NG):
                            pe.wait_ge(gen_ready, 2 * (k * GEN + j * NG + g + 1))
                            pe.wait_ge(gen_gathered[g], SIZES[g] * 16 * (k * NI + j + 1))
                            sum_group(g, SIZES[g], gen_summed)
                    with pe.Fori(0, ET) as q:
                        pe.wait_ge(gen_ready, 2 * (k * GEN + NI * NG + q + 1))
                        pe.wait_ge(gen_gathered_early, 16 * (k * ET + q + 1))
                        sum_group(0, 1, gen_summed)
                with pe.Fori(0, NT) as j:
                    finish_turn(j + NA)
                    finish_linear(j + NA)


_INS = ["x", "src", "dst", "edge_type_3", "node_type_3", "L0_gnn_W_e", "L0_gnn_b_e", "L0_gnn_W_n", "L0_gnn_b_n"]


def kernel(**inputs):
    import numpy as np
    import concourse.bacc as bacc
    from concourse import mybir
    from concourse.bass_utils import run_bass_kernel_spmd

    nc = bacc.Bacc("TRN2", target_bir_lowering=False, num_devices=1)
    arrays, args = {}, []
    for name in _INS:
        a = np.ascontiguousarray(inputs[name])
        arrays[f"in_{name}"] = a
        args.append(nc.dram_tensor(f"in_{name}", a.shape, mybir.dt.from_np(a.dtype), kind="ExternalInput").ap())
    out = nc.dram_tensor("out_0", (6250, 128), mybir.dt.float32, kind="ExternalOutput").ap()
    build(nc, *args, out)
    r = run_bass_kernel_spmd(nc, [arrays], core_ids=[0])
    return r.results[0]["out_0"]
```
